# Optimizing a Trainium2 kernel written in Bass

```python
import numpy as np
import jax
import jax.numpy as jnp

def _softmax(x, axis=-1):
    return jax.nn.softmax(x, axis=axis)

def _gelu(x):
    return jax.nn.gelu(x, approximate=True)

def _silu(x):
    return jax.nn.silu(x)

def _sigmoid(x):
    return jax.nn.sigmoid(x)

def _layernorm(x, axis=-1, eps=1e-05):
    m = jnp.mean(x, axis=axis, keepdims=True)
    v = jnp.var(x, axis=axis, keepdims=True)
    return (x - m) / jnp.sqrt(v + eps)

def _scatter_add(tgt, idx, src, axis=0):
    return tgt.at[idx].add(src)

def _segment_sum(src, seg, n):
    return jax.ops.segment_sum(src, seg, n)
kernel_name = 'mk_flamingo_gated_d1_seqx_r4_c52141'

def setup_inputs(seed: int=0):
    np.random.seed(seed)
    _w = jnp.asarray

    def _rec_inputs():
        import jax
        import jax.numpy as jnp
        _rk = jax.random.key(seed)
        x = 7.22e-05 + 1 * jax.random.normal(jax.random.fold_in(_rk, 1), (8, 256, 512), jnp.float32)
        _lenS = 256 - jax.random.randint(jax.random.fold_in(_rk, 7), (8,), 0, max(1, 256 // 4) + 1, jnp.int32)
        _lenS2 = 256 - jax.random.randint(jax.random.fold_in(_rk, 8), (8,), 0, max(1, 256 // 4) + 1, jnp.int32)
        _ctx_512P = jax.random.normal(jax.random.fold_in(_rk, 11), (8, 16, 128), jnp.float32)
        _ctx_512c = jax.random.dirichlet(jax.random.fold_in(_rk, 511), 0.3 * jnp.ones((16,), jnp.float32), (8, 256))
        _ctx_512t = jnp.einsum('bsk,bkd->bsd', _ctx_512c, _ctx_512P)
        _ctx_512t = _ctx_512t * jax.lax.rsqrt(jnp.mean(jnp.square(_ctx_512t)) + 1e-12) * 0.953939
        ctx_512 = -0.000514642 + 1.00011 * (_ctx_512t + 0.3 * jax.random.normal(jax.random.fold_in(_rk, 611), (8, 256, 128), jnp.float32))
        _g = jax.random.normal(jax.random.fold_in(_rk, 9001), (2, 1), jnp.float32)
        _g = jnp.sign(_g) * jnp.maximum(jnp.abs(_g), 1.0) + (_g == 0) * 1.0
        g_xattn = _g[0]
        g_ffn = _g[1]
        return (x, ctx_512, g_xattn, g_ffn)
    x, ctx_512, g_xattn, g_ffn = _rec_inputs()

    def _L0_xattn_setup():
        import jax, jax.numpy as jnp
        import numpy as np
        import math
        NUM_Q_HEADS = 32
        NUM_KV_HEADS = 8
        key = jax.random.key(seed)
        k1, k2, k3 = jax.random.split(key, 3)
        B, S, E = (2, 512, 512)
        kv_E = NUM_KV_HEADS * (E // NUM_Q_HEADS)
        q = jax.random.normal(k1, (B, S, E), dtype=jnp.float32)
        k = jax.random.normal(k2, (B, S, kv_E), dtype=jnp.float32)
        v = jax.random.normal(k3, (B, S, kv_E), dtype=jnp.float32)
        return {'q': q, 'k': k, 'v': v}
    _L0_xattn_all = _L0_xattn_setup()
    _L0_xattn_in = {k: v for k, v in _L0_xattn_all.items() if k in ()}
    del _L0_xattn_all

    def _L0_ffn_setup():
        import jax, jax.numpy as jnp
        import numpy as np
        HIDDEN = 512
        INTER = 1408
        B, S = (2, 512)

        def _ternary(key, shape):
            return jax.random.randint(key, shape, -1, 2).astype(jnp.float32)
        key = jax.random.key(seed)
        ks = jax.random.split(key, 7)
        x = jax.random.normal(ks[0], (B, S, HIDDEN), dtype=jnp.float32)
        gate_w = _ternary(ks[1], (INTER, HIDDEN))
        up_w = _ternary(ks[2], (INTER, HIDDEN))
        down_w = _ternary(ks[3], (HIDDEN, INTER))
        gate_s = jax.random.uniform(ks[4], (INTER,), minval=0.01, maxval=0.1, dtype=jnp.float32)
        up_s = jax.random.uniform(ks[5], (INTER,), minval=0.01, maxval=0.1, dtype=jnp.float32)
        down_s = jax.random.uniform(ks[6], (HIDDEN,), minval=0.01, maxval=0.1, dtype=jnp.float32)
        return {'x': x, 'gate_w': gate_w, 'up_w': up_w, 'down_w': down_w, 'gate_s': gate_s, 'up_s': up_s, 'down_s': down_s}
    _L0_ffn_all = _L0_ffn_setup()
    _L0_ffn_in = {k: v for k, v in _L0_ffn_all.items() if k in ('gate_w', 'up_w', 'down_w', 'gate_s', 'up_s', 'down_s')}
    del _L0_ffn_all
    return {'x': x, 'ctx_512': ctx_512, 'g_xattn': g_xattn, 'g_ffn': g_ffn, 'L0_ffn_gate_w': _L0_ffn_in['gate_w'], 'L0_ffn_up_w': _L0_ffn_in['up_w'], 'L0_ffn_down_w': _L0_ffn_in['down_w'], 'L0_ffn_gate_s': _L0_ffn_in['gate_s'], 'L0_ffn_up_s': _L0_ffn_in['up_s'], 'L0_ffn_down_s': _L0_ffn_in['down_s']}

def reference(x, ctx_512, g_xattn, g_ffn, L0_ffn_gate_w, L0_ffn_up_w, L0_ffn_down_w, L0_ffn_gate_s, L0_ffn_up_s, L0_ffn_down_s):
    import jax
    import jax.numpy as jnp

    def _L0_xattn_ref(q, k, v):
        import jax, jax.numpy as jnp
        import numpy as np
        import math
        NUM_Q_HEADS = 32
        NUM_KV_HEADS = 8
        B, S, E = q.shape
        H, KV = (NUM_Q_HEADS, NUM_KV_HEADS)
        D = E // H
        G = H // KV
        scale = math.sqrt(D)
        qh = q.reshape(B, S, KV, G, D).transpose(0, 2, 3, 1, 4)
        kh = k.reshape(B, S, KV, D).transpose(0, 2, 1, 3)
        vh = v.reshape(B, S, KV, D).transpose(0, 2, 1, 3)
        scores = jnp.einsum('bkgsd,bktd->bkgst', qh, kh) / scale
        weights = jax.nn.softmax(scores, axis=-1)
        out = jnp.einsum('bkgst,bktd->bkgsd', weights, vh)
        return out.transpose(0, 3, 1, 2, 4).reshape(B, S, E)

    def _L0_ffn_ref(x, gate_w, up_w, down_w, gate_s, up_s, down_s):
        import jax, jax.numpy as jnp
        import numpy as np
        HIDDEN = 512
        INTER = 1408
        B, S = (2, 512)

        def _ternary(key, shape):
            return jax.random.randint(key, shape, -1, 2).astype(jnp.float32)
        b, s, h = x.shape
        xf = x.reshape(b * s, h)
        g = jnp.einsum('th,ih->ti', xf, gate_w) * gate_s
        u = jnp.einsum('th,ih->ti', xf, up_w) * up_s
        hdn = jax.nn.silu(g) * u
        out = jnp.einsum('ti,hi->th', hdn, down_w) * down_s
        return out.reshape(b, s, -1)
    x = x + jnp.tanh(g_xattn[0]) * _L0_xattn_ref(_layernorm(x, axis=-1), ctx_512, ctx_512)
    x = x + jnp.tanh(g_ffn[0]) * _L0_ffn_ref(_layernorm(x, axis=-1), L0_ffn_gate_w, L0_ffn_up_w, L0_ffn_down_w, L0_ffn_gate_s, L0_ffn_up_s, L0_ffn_down_s)
    return x

_drawn_inputs = setup_inputs


def setup_inputs(seed=0):
    import zlib

    import numpy as np

    out = dict(_drawn_inputs(seed))
    spreads = {}
    factors = {}
    for name, (base, spread) in spreads.items():
        noise = np.random.default_rng([zlib.crc32(name.encode()), seed]).standard_normal(out[name].shape)
        drawn = base * np.exp(spread * noise) if base else spread * noise
        out[name] = jnp.asarray(drawn.astype(out[name].dtype))
    for name, factor in factors.items():
        out[name] = (out[name] * factor).astype(out[name].dtype)
    return out
```

```python
import numpy as np
import concourse.bass as bass
from concourse import mybir
from contextlib import ExitStack

F32 = mybir.dt.float32
F32R = mybir.dt.float32r
I32 = mybir.dt.int32
ALU = mybir.AluOpType
ACT = mybir.ActivationFunctionType
AX = mybir.AxisListType

P = 128
B, S, E = 8, 256, 512
T = 256
H, KV, D = 32, 8, 16
G = H // KV
ST = S // P
TT = T // P
UNITS = 4
PAIRS, UG = 4, 2
UH = PAIRS * UG
UKV = KV // 2
NPART = 4
ZROW = NPART * D
HIROW, LOROW = ZROW + 1, ZROW + 2
SROWS, DROWS = ZROW + 1, ZROW + 3
VW = 32
F = 1408
IT = F // P
KT = E // P
CH = 512
CT = CH // P
NCH = B * S // CH
HS = 3
LAG = 2
WCOLS = 3 * KT * F
WPIECES = 6
WP = WCOLS // WPIECES
WQ = WP // UNITS
EPS = 1e-5
LOW_BITS = 0xFFF
RSCALE = 1.0 / float(D) ** 0.5


def kv_of(k, pair):
    return (k % 2) * 2 + pair // 2


def build(nc, x, ctx_n, ctx_t, g_xattn, g_ffn, weights, gate_s, up_s, down_s, out):
    q_parts = nc.dram_tensor("q_parts", [B, UNITS, UH, 2, D, S], F32).ap()
    x1_dram = nc.dram_tensor("x1_scratch", [B * S, E], F32).ap()

    with ExitStack() as top:
        def sem(name):
            return top.enter_context(nc.semaphore(name))

        def sb(stack, name, shape, dt=F32):
            return stack.enter_context(nc.sbuf_tensor(name, shape, dt))

        def ps(stack, name, shape, dt=F32):
            return stack.enter_context(nc.psum_tensor(name, shape, dt))

        w_sb = sb(top, "w_sb", [P, WCOLS], F32R)
        ident = sb(top, "ident", [P, P])
        ident_zero = sb(top, "ident_zero", [P, P])
        gates = sb(top, "gates", [P, 2])
        tgates = sb(top, "tgates", [P, 2])
        gs_col = sb(top, "gs_col", [P, IT])
        us_col = sb(top, "us_col", [P, IT])
        half_gs = sb(top, "half_gs", [P, IT])
        hid_scale = sb(top, "hid_scale", [P, IT])
        down_row = sb(top, "down_row", [P, E])
        down_gate = sb(top, "down_gate", [P, E])
        bits = sb(top, "bits", [P, WQ], I32)
        low_bits = sb(top, "low_bits", [P, WQ], I32)
        low_col = sb(top, "low_col", [P, 1])
        low_flag = sb(top, "low_flag", [1, 1], I32)
        minus_half = sb(top, "minus_half", [P, CT])
        stats = sb(top, "stats", [P, CT, 6])
        moments = sb(top, "moments", [P, CT, 2])
        var_eps = sb(top, "var_eps", [P, CT])
        rstd = sb(top, "rstd", [P, CT])
        mean_rstd = sb(top, "mean_rstd", [P, CT])
        shift = sb(top, "shift", [P, CT])

        att = ExitStack()
        q_st = [sb(att, f"q_st{k}", [DROWS, UH, S], F32R) for k in range(UNITS)]
        k_max = [sb(att, f"k_max{h}", [DROWS, UKV, T], F32R) for h in range(2)]
        k_exp = [sb(att, f"k_exp{h}", [DROWS, UKV, T], F32R) for h in range(2)]
        k_raw = sb(att, "k_raw", [ZROW, KV, T])
        v_raw = sb(att, "v_raw", [P, TT, KV * D])
        v_aug = [sb(att, f"v_aug{h}", [P, TT, UKV, VW]) for h in range(2)]
        probs = sb(att, "probs", [P, TT, PAIRS, UG * S])
        o_sb = sb(att, "o_sb", [P, UG * S])
        attn = sb(att, "attn", [P, ST, E])
        rden = sb(att, "rden", [P, UG * ST, PAIRS])
        negmax = [sb(att, f"negmax{h}", [P, UH * ST]) for h in range(2)]
        m_hi = [sb(att, f"m_hi{h}", [UH * ST, P], F32R) for h in range(2)]
        m_lo = [sb(att, f"m_lo{h}", [UH * ST, P], F32R) for h in range(2)]
        x_ln = sb(att, "x_ln", [P, ST, E])
        x_norm = sb(att, "x_norm", [P, ST, E])
        qt_hi = [sb(att, f"qt_hi{h}", [P, 2, S], F32R) for h in range(2)]
        qt_lo = [sb(att, f"qt_lo{h}", [P, 2, S], F32R) for h in range(2)]
        x_res = sb(att, "x_res", [P, ST, E])
        w_stage = sb(att, "w_stage", [P, WP])
        s_ps = [ps(att, f"s_ps{h}", [P, 2 * ST, T]) for h in range(2)]
        t_ps = [ps(att, f"t_ps{h}", [P, UG * S]) for h in range(2)]
        o_ps = ps(att, "o_ps", [P, UG * S])
        tr_ps = ps(att, "tr_ps", [P, 2 * S])
        att.close()

        ffn = ExitStack()
        c_ln = sb(ffn, "c_ln", [P, CT, E])
        c_norm = sb(ffn, "c_norm", [P, CT, E])
        c_res = sb(ffn, "c_res", [P, CT, E])
        xt_hi = sb(ffn, "xt_hi", [P, KT, CH], F32R)
        xt_lo = sb(ffn, "xt_lo", [P, KT, CH], F32R)
        th = [sb(ffn, f"th{h}", [P, CH]) for h in range(2)]
        silu2 = [sb(ffn, f"silu2{h}", [P, CH]) for h in range(2)]
        hid = [sb(ffn, f"hid{h}", [P, CH]) for h in range(HS)]
        hid_hi = [sb(ffn, f"hid_hi{h}", [P, CH], F32R) for h in range(HS)]
        hid_lo = [sb(ffn, f"hid_lo{h}", [P, CH], F32R) for h in range(HS)]
        y_sb = sb(ffn, "y_sb", [P, CT, E])
        gu_ps = [ps(ffn, f"gu_ps{h}", [P, 2, CH]) for h in range(2)]
        acc_ps = [ps(ffn, f"acc_ps{t}", [P, E]) for t in range(CT)]
        ffn.close()

        gates_in = sem("gates_in")
        scales_in = sem("scales_in")
        filled = sem("filled")
        padded = sem("padded")
        ident_done = sem("ident_done")
        tanh_done = sem("tanh_done")
        scales_done = sem("scales_done")
        x_in = sem("x_in")
        stat_done = sem("stat_done")
        moments_done = sem("moments_done")
        norm_chain = sem("norm_chain")
        x_normed = sem("x_normed")
        qt_turned = sem("qt_turned")
        qt_hi_done = sem("qt_hi_done")
        qt_lo_done = sem("qt_lo_done")
        qt_stored = [sem(f"qt_stored{h}") for h in range(2)]
        q_in = [sem(f"q_in{k}") for k in range(UNITS)]
        k_in = sem("k_in")
        k_hi_done = sem("k_hi_done")
        k_max_done = sem("k_max_done")
        k_exp_done = sem("k_exp_done")
        v_in = sem("v_in")
        v_done = sem("v_done")
        s_done = sem("s_done")
        max_done = sem("max_done")
        m_turned = sem("m_turned")
        m_hi_done = sem("m_hi_done")
        m_lo_done = sem("m_lo_done")
        m_in = sem("m_in")
        t_done = sem("t_done")
        exp_done = sem("exp_done")
        pv_done = sem("pv_done")
        o_copied = sem("o_copied")
        o_turned = sem("o_turned")
        rden_done = sem("rden_done")
        o_normed = sem("o_normed")
        r_in = sem("r_in")
        gated_done = sem("gated_done")
        x1_done = sem("x1_done")
        x1_stored = sem("x1_stored")
        w_in = sem("w_in")
        w_seen = sem("w_seen")
        w_set = sem("w_set")
        flag_step = sem("flag_step")
        flag_turned = sem("flag_turned")
        flag_done = sem("flag_done")
        c_in = sem("c_in")
        c_normed = sem("c_normed")
        c_turned = sem("c_turned")
        c_hi_done = sem("c_hi_done")
        c_lo_done = sem("c_lo_done")
        gu_done = sem("gu_done")
        th_done = sem("th_done")
        silu_done = sem("silu_done")
        hid_done = sem("hid_done")
        hid_hi_done = sem("hid_hi_done")
        hid_lo_done = sem("hid_lo_done")
        down_done = sem("down_done")
        y_done = sem("y_done")
        cr_in = sem("cr_in")
        out_ready = sem("out_ready")
        out_stored = sem("out_stored")

        sp_passed, pool_passed, dve_passed = sem("sp_passed"), sem("pool_passed"), sem("dve_passed")

        block = top.enter_context(nc.Block())

        kt_view = ctx_t.rearrange("(v d) (b t) -> b d v t", d=D, b=B)
        v_view = ctx_n.rearrange("b (tt p) e -> b p tt e", p=P)
        x_view = x.rearrange("b (st p) e -> b p st e", p=P)
        x1w_view = x1_dram.rearrange("(b st p) e -> b p st e", p=P, st=ST)
        x1c_view = x1_dram.rearrange("(c ct p) e -> c p ct e", p=P, ct=CT)
        out_view = out.rearrange("b s e -> (b s) e").rearrange("(c ct p) e -> c p ct e", p=P, ct=CT)
        gate_w = w_sb[:, 0:KT * F].rearrange("p (k i) -> p k i", k=KT)
        up_w = w_sb[:, KT * F:2 * KT * F].rearrange("p (k i) -> p k i", k=KT)
        down_w = w_sb[:, 2 * KT * F:WCOLS].rearrange("p (i h) -> p i h", i=IT)
        attn_units = attn[:, :, :].rearrange("p st (k i g d) -> p k g st i d", k=UNITS, i=PAIRS, g=UG)

        def waited(engine, passed):
            engine.sem_inc(passed)

        LAST = B - 1
        NORMS = B - 2

        @block.sync
        def _(sp):
            def load_x(b):
                sp.dma_start(x_ln[:, :, :], x_view[b]).then_inc(x_in, 16)

            def load_k(b):
                for r in range(NPART):
                    sp.dma_start(k_raw[r * D:(r + 1) * D, :, :], kt_view[b]).then_inc(k_in, 16)

            def load_v(b):
                sp.dma_start(v_raw[:, :, :], v_view[b]).then_inc(v_in, 16)

            def store_q(b, c):
                sp.wait_ge(qt_lo_done, 2 * b + c + 1)
                for part, tile in ((0, qt_hi[c]), (1, qt_lo[c])):
                    for j in range(2):
                        sp.dma_start(q_parts[b, 2 * c + j, :, part, :, :], tile[:, j, :].bitcast(F32)).then_inc(qt_stored[c], 16)

            def load_q(b, k, reused):
                sp.wait_ge(qt_stored[k // 2], 64 * (b + 1))
                if reused:
                    waited(sp, sp_passed)
                    sp.wait_ge(t_done, 2 * PAIRS * (UNITS * (b - 1) + k + 1))
                waited(sp, sp_passed)
                src = q_parts[b, k].rearrange("h part d s -> (part d) h s")
                for r in range(2):
                    sp.dma_start(q_st[k][r * 2 * D:(r + 1) * 2 * D, :, :].bitcast(F32), src).then_inc(q_in[k], 16)

            def place_maxima(b, k):
                sp.wait_ge(m_lo_done, UNITS * b + k + 1)
                for row, tile in ((HIROW, m_hi[k % 2]), (LOROW, m_lo[k % 2])):
                    sp.dma_start(q_st[k][row:row + 1, :, :].bitcast(F32), tile[:, :].bitcast(F32)).then_inc(m_in, 16)

            load_x(0)
            sp.dma_start(gates[:, 0:1], g_xattn.partition_broadcast(P)).then_inc(gates_in, 16)
            sp.dma_start(gates[:, 1:2], g_ffn.partition_broadcast(P)).then_inc(gates_in, 16)
            load_k(0)
            load_v(0)
            sp.wait_ge(x_normed, ST)
            load_x(1)
            for c in range(2):
                store_q(0, c)
            for k in range(3):
                load_q(0, k, False)
            sp.wait_ge(k_max_done, 2)
            load_k(1)
            sp.wait_ge(x_normed, 2 * ST)
            load_x(2)
            for c in range(2):
                store_q(1, c)
            sp.dma_start(gs_col[:, :], gate_s).then_inc(scales_in, 16)
            sp.dma_start(us_col[:, :], up_s).then_inc(scales_in, 16)
            sp.dma_start(down_row[:, :], down_s.partition_broadcast(P)).then_inc(scales_in, 16)
            place_maxima(0, 0)

            def step(b, k, first, last):
                norming = not last and b is not NORMS
                if k == 0:
                    load_q(b, 3, not first)
                elif not last:
                    load_q(b + 1, k - 1, True)
                if k < 3:
                    place_maxima(b, k + 1)
                elif not last:
                    place_maxima(b + 1, 0)
                if k == 2 and not last:
                    sp.wait_ge(v_done, 2 * TT * (b + 1))
                    load_v(b + 1)
                if k == 1:
                    if not first:
                        sp.wait_ge(x1_done, b)
                        sp.dma_start(x1w_view[b - 1], x_res[:, :, :]).then_inc(x1_stored, 16)
                        sp.wait_ge(x1_stored, 16 * b)
                    sp.dma_start(x_res[:, :, :], x_view[b]).then_inc(r_in, 16)
                if k == 2 and norming:
                    sp.wait_ge(k_max_done, 2 * (b + 2))
                    load_k(b + 2)
                if norming:
                    if k == 0:
                        if not first:
                            sp.wait_ge(w_set, 16 * b)
                            sp.wait_ge(w_seen, UNITS * b)
                        sp.dma_start(w_stage[:, :], weights[:, bass.ds(b * WP, WP)]).then_inc(w_in, 16)
                    if k == 1:
                        sp.wait_ge(w_in, 16 * (b + 1))
                        waited(sp, sp_passed)
                        sp.dma_start(w_sb[:, bass.ds(b * WP, WP)].bitcast(F32), w_stage[:, :]).then_inc(w_set, 16)
                    if k >= 2:
                        store_q(b + 2, k - 2)

            def next_x(b, k):
                if k == 2:
                    sp.wait_ge(x_normed, ST * (b + 3))
                    load_x(b + 3)

            for k in range(UNITS):
                step(0, k, True, False)
                next_x(0, k)
            with sp.Fori(1, NORMS - 1) as b:
                for k in range(UNITS):
                    step(b, k, False, False)
                    next_x(b, k)
            for b in (NORMS - 1, NORMS, LAST):
                for k in range(UNITS):
                    step(b, k, False, b == LAST)
            sp.wait_ge(x1_done, B)
            sp.dma_start(x1w_view[LAST], x_res[:, :, :]).then_inc(x1_stored, 16)

            sp.wait_ge(x1_stored, 16 * B)

            def load_chunk(c):
                sp.dma_start(c_ln[:, :, :], x1c_view[c]).then_inc(c_in, 16)

            def load_residual(c):
                sp.dma_start(c_res[:, :, :], x1c_view[c]).then_inc(cr_in, 16)

            def store_out(c):
                for t in range(CT):
                    sp.wait_ge(out_ready, CT * c + t + 1)
                    sp.dma_start(out_view[c, :, t, :], y_sb[:, t, :]).then_inc(out_stored, 16)

            load_chunk(0)
            load_residual(0)
            with sp.Fori(0, NCH - 1) as c:
                sp.wait_ge(c_normed, CT * (c + 1))
                load_chunk(c + 1)
                store_out(c)
                sp.wait_ge(out_stored, 16 * CT * (c + 1))
                load_residual(c + 1)
            store_out(NCH - 1)
            sp.wait_ge(out_stored, 16 * CT * NCH)

        @block.gpsimd
        def _(pool):
            pool.memset(ident_zero[:, :], 0.0).then_inc(filled, 1)
            pool.wait_ge(filled, 1)
            pool.affine_select(out=ident[:, :], in_=ident_zero[:, :], compare_op=ALU.not_equal, fill=1.0, base=0,
                               pattern=[[-1, P]], channel_multiplier=1).then_inc(ident_done, 1)
            pool.memset(minus_half[:, :], -0.5).then_inc(filled, 1)

            def norm_tiles(rows, n, src, dst, tiles, done):
                pool.wait_ge(moments_done, tiles)
                waited(pool, pool_passed)
                pool.tensor_scalar(var_eps[:, 0:n], moments[:, 0:n, 1], 1.0, EPS, ALU.mult, ALU.add).then_inc(norm_chain, 1)
                pool.wait_ge(norm_chain, 4 * rows + 1)
                pool.tensor_tensor(rstd[:, 0:n], var_eps[:, 0:n], minus_half[:, 0:n], ALU.pow).then_inc(norm_chain, 1)
                pool.wait_ge(norm_chain, 4 * rows + 2)
                pool.tensor_tensor(mean_rstd[:, 0:n], moments[:, 0:n, 0], rstd[:, 0:n], ALU.mult).then_inc(norm_chain, 1)
                pool.wait_ge(norm_chain, 4 * rows + 3)
                waited(pool, pool_passed)
                pool.tensor_scalar(shift[:, 0:n], mean_rstd[:, 0:n], -1.0, 0.0, ALU.mult, ALU.add).then_inc(norm_chain, 1)
                pool.wait_ge(norm_chain, 4 * rows + 4)
                waited(pool, pool_passed)
                for t in range(n):
                    pool.tensor_scalar(dst[:, t, :], src[:, t, :], rstd[:, t:t + 1], shift[:, t:t + 1],
                                       ALU.mult, ALU.add).then_inc(done, 1)

            def norm_batch(b, reused):
                if reused:
                    pool.wait_ge(qt_turned, 2 * b)
                norm_tiles(b, ST, x_ln, x_norm, ST * (b + 1), x_normed)

            def keys_for_max(b, h, reused):
                n = 2 * b + h
                pool.wait_ge(k_in, 16 * NPART * (b + 1))
                if reused:
                    pool.wait_ge(s_done, PAIRS * (UNITS * (b - 1) + 2 * h + 2))
                    pool.wait_ge(k_exp_done, 2 * (b - 1) + h + 1)
                waited(pool, pool_passed)
                raw = k_raw[:, h * UKV:(h + 1) * UKV, :]
                half = slice(ZROW // 2, ZROW)
                pool.tensor_scalar(k_max[h][0:ZROW, :, :], raw, 1.0, 0.0, ALU.mult, ALU.add).then_inc(k_hi_done, 1)
                pool.wait_ge(k_hi_done, n + 1)
                pool.tensor_tensor(k_max[h][half, :, :], raw[half, :, :],
                                   k_max[h][half, :, :].bitcast(F32), ALU.subtract).then_inc(k_max_done, 1)
                pool.wait_ge(k_max_done, n + 1)

            def keys_for_exp(b, h, reused):
                pool.wait_ge(k_max_done, 2 * b + h + 1)
                if reused:
                    pool.wait_ge(t_done, 2 * PAIRS * (UNITS * (b - 1) + 2 * h + 2))
                waited(pool, pool_passed)
                pool.tensor_scalar(k_exp[h][0:ZROW, :, :], k_max[h][0:ZROW, :, :].bitcast(F32), 1.0, 0.0,
                                   ALU.mult, ALU.add).then_inc(k_exp_done, 1)

            def values(b, h, reused):
                pool.wait_ge(v_in, 16 * (b + 1))
                if reused:
                    pool.wait_ge(pv_done, TT * (UNITS * (b - 1) + 2 * h + 2))
                waited(pool, pool_passed)
                for tt in range(TT):
                    src = v_raw[:, tt, h * UKV * D:(h + 1) * UKV * D].rearrange("p (v d) -> p v d", d=D)
                    pool.tensor_scalar(v_aug[h][:, tt, :, 0:D], src, 1.0, 0.0, ALU.mult, ALU.add).then_inc(v_done, 1)

            def residual(b):
                pool.wait_ge(o_normed, UNITS * (b + 1))
                waited(pool, pool_passed)
                pool.tensor_scalar(attn[:, :, :], attn[:, :, :], tgates[:, 0:1], 0.0,
                                   ALU.mult, ALU.add).then_inc(gated_done, 1)
                pool.wait_ge(gated_done, b + 1)
                pool.wait_ge(r_in, 16 * (b + 1))
                pool.tensor_tensor(x_res[:, :, :], x_res[:, :, :], attn[:, :, :], ALU.add).then_inc(x1_done, 1)

            pool.wait_ge(filled, 2)
            norm_batch(0, False)
            pool.wait_ge(padded, UNITS + 8)
            for h in range(2):
                keys_for_max(0, h, False)
                keys_for_exp(0, h, False)
            for h in range(2):
                values(0, h, False)
            norm_batch(1, True)
            pool.wait_ge(tanh_done, 1)

            def step(b, k, first, last):
                if k == 0:
                    if not last:
                        keys_for_max(b + 1, 0, True)
                    if not first:
                        keys_for_exp(b, 1, True)
                        residual(b - 1)
                if k == 1:
                    if not first:
                        values(b, 1, True)
                    if not last and b is not NORMS:
                        norm_batch(b + 2, True)
                if k == 2 and not last:
                    keys_for_max(b + 1, 1, True)
                    keys_for_exp(b + 1, 0, True)
                if k == 3 and not last:
                    values(b + 1, 0, True)

            for k in range(UNITS):
                step(0, k, True, False)
            with pool.Fori(1, NORMS) as b:
                for k in range(UNITS):
                    step(b, k, False, False)
            for b in (NORMS, LAST):
                for k in range(UNITS):
                    step(b, k, False, b == LAST)
            residual(LAST)

            pool.wait_ge(x1_stored, 16 * B)

            def norm_chunk(c, reused):
                pool.wait_ge(c_in, 16 * (c + 1))
                if reused:
                    pool.wait_ge(c_turned, 2 * c)
                norm_tiles(B + c, CT, c_ln, c_norm, ST * B + CT * (c + 1), c_normed)

            def hidden_low(n, slot):
                pool.wait_ge(hid_hi_done, n + 1)
                pool.tensor_tensor(hid_lo[slot][:, :], hid[slot][:, :], hid_hi[slot][:, :].bitcast(F32),
                                   ALU.subtract).then_inc(hid_lo_done, 1)

            def add_residual(c, t):
                pool.wait_ge(y_done, CT * c + t + 1)
                pool.wait_ge(cr_in, 16 * (c + 1))
                pool.tensor_tensor(y_sb[:, t, :], y_sb[:, t, :], c_res[:, t, :], ALU.add).then_inc(out_ready, 1)

            def chunk(c, last):
                for i in range(2, IT):
                    hidden_low(IT * c + i, i % HS)
                    if i == 7 and not last:
                        norm_chunk(c + 1, True)
                if last:
                    for t in range(CT):
                        add_residual(c, t)
                else:
                    add_residual(c, 0)
                    add_residual(c, 1)
                    hidden_low(IT * (c + 1), 0)
                    add_residual(c, 2)
                    hidden_low(IT * (c + 1) + 1, 1)
                    add_residual(c, 3)

            norm_chunk(0, False)
            hidden_low(0, 0)
            hidden_low(1, 1)
            with pool.Fori(0, NCH - 1) as c:
                chunk(c, False)
            chunk(NCH - 1, True)

        @block.vector
        def _(dve):
            for k in range(UNITS):
                dve.memset(q_st[k][ZROW:SROWS, :, :].bitcast(F32), 0.0).then_inc(padded, 1)
            for h in range(2):
                dve.memset(k_max[h][ZROW:DROWS, :, :].bitcast(F32), 1.0).then_inc(padded, 1)
                dve.memset(k_exp[h][ZROW:DROWS, :, :].bitcast(F32), 1.0).then_inc(padded, 1)
                dve.memset(v_aug[h][:, :, :, D + 1:VW], 0.0).then_inc(padded, 1)
                dve.memset(v_aug[h][:, :, :, D:D + 1], 1.0).then_inc(padded, 1)

            dve.memset(bits[:, :], 0).then_inc(padded, 1)
            dve.wait_ge(padded, UNITS + 9)

            def tile_moments(src, t, n, col):
                dve.bn_stats(stats[:, t, :], src[:, t, :]).then_inc(stat_done, 1)
                dve.wait_ge(stat_done, n + 1)
                waited(dve, dve_passed)
                dve.bn_aggr(moments[:, t, :], stats[:, t, :]).then_inc(moments_done, 1)

            def batch_moments(b, t, reused):
                dve.wait_ge(x_in, 16 * (b + 1))
                if reused:
                    dve.wait_ge(x_normed, ST * b)
                tile_moments(x_ln, t, ST * b + t, t)

            def queries_low(b, c, reused):
                dve.wait_ge(qt_hi_done, 2 * b + c + 1)
                if reused:
                    dve.wait_ge(qt_stored[c], 64 * b)
                dve.tensor_tensor(qt_lo[c][:, :, :], tr_ps[:, :].rearrange("p (j s) -> p j s", j=2),
                                  qt_hi[c][:, :, :].bitcast(F32), ALU.subtract).then_inc(qt_lo_done, 1)

            def maxima(b, k, t, reused):
                u = UNITS * b + k
                dve.wait_ge(s_done, PAIRS * u + t + 1)
                if t == 0 and reused:
                    dve.wait_ge(m_turned, u - 1)
                dve.tensor_reduce(negmax[k % 2][:, 4 * t:4 * t + 4], s_ps[t % 2][:, :, :], AX.X, ALU.max,
                                  negate=True).then_inc(max_done, 1)

            def maxima_low(u, k):
                dve.wait_ge(m_hi_done, u + 1)
                dve.tensor_tensor(m_lo[k % 2][:, :], tr_ps[0:UH * ST, 0:P], m_hi[k % 2][:, :].bitcast(F32),
                                  ALU.subtract).then_inc(m_lo_done, 1)

            def divide(u, k):
                dve.wait_ge(o_turned, u + 1)
                turned = tr_ps[:, :].rearrange("p (j i w) -> p j i w", j=UG * ST, i=PAIRS)
                dve.reciprocal(rden[:, :, :], turned[:, :, :, D]).then_inc(rden_done, 1)
                dve.wait_ge(rden_done, u + 1)
                for g in range(UG):
                    mul = dve.tensor_tensor(attn_units[:, k, g], turned[:, ST * g:ST * g + ST, :, 0:D],
                                            rden[:, ST * g:ST * g + ST, :].unsqueeze(3).broadcast_to([P, ST, PAIRS, D]),
                                            ALU.mult)
                mul.then_inc(o_normed, 1)

            for t in range(ST):
                batch_moments(0, t, False)
            for c in range(2):
                queries_low(0, c, False)
            for t in range(ST):
                batch_moments(1, t, t == 0)
            for c in range(2):
                queries_low(1, c, True)
            for k in range(2):
                for t in range(4):
                    maxima(0, k, t, False)
                if k == 1:
                    maxima_low(0, 0)
            dve.wait_ge(scales_in, 48)
            dve.tensor_scalar(half_gs[:, :], gs_col[:, :], 0.5, None, ALU.mult).then_inc(scales_done, 1)
            dve.wait_ge(scales_done, 1)
            dve.tensor_tensor(hid_scale[:, :], half_gs[:, :], us_col[:, :], ALU.mult).then_inc(scales_done, 1)
            dve.wait_ge(tanh_done, 1)
            dve.tensor_scalar(down_gate[:, :], down_row[:, :], tgates[:, 1:2], None, ALU.mult).then_inc(scales_done, 1)

            def step(b, k, first, last):
                u = UNITS * b + k
                norming = not last and b is not NORMS
                ahead = (b, k + 2) if k < 2 else (b + 1, k - 2)
                for t in range(4):
                    if not (last and k >= 2):
                        maxima(*ahead, t, True)
                    if t == 0 and not (last and k == 3):
                        maxima_low(u + 1, k + 1)
                    if t == 1 and norming and k >= 2:
                        queries_low(b + 2, k - 2, True)
                    if t == 1 and b is NORMS and k == 2:
                        dve.wait_ge(flag_turned, 1)
                        dve.tensor_reduce(low_flag[:, :], tr_ps[0:1, 0:P], AX.X, ALU.max).then_inc(flag_done, 1)
                    if t == 1 and norming and k < 2:
                        batch_moments(b + 2, k, k == 0)
                    if t == 2 and not (first and k == 0):
                        if k == 1 and not first:
                            dve.wait_ge(x1_done, b)
                        divide(u - 1, (k - 1) % UNITS)
                if norming:
                    dve.wait_ge(w_in, 16 * (b + 1))
                    if not (first and k == 0):
                        dve.wait_ge(w_seen, UNITS * b + k)
                    dve.tensor_tensor(bits[:, :], bits[:, :], w_stage[:, k * WQ:(k + 1) * WQ].bitcast(I32),
                                      ALU.bitwise_or).then_inc(w_seen, 1)
                if b is NORMS and k == 0:
                    dve.wait_ge(w_seen, WPIECES * UNITS)
                    dve.tensor_scalar(low_bits[:, :], bits[:, :], LOW_BITS, None, ALU.bitwise_and).then_inc(flag_step, 1)
                    dve.wait_ge(flag_step, 1)
                    dve.tensor_reduce(low_col[:, :], low_bits[:, :], AX.X, ALU.max).then_inc(flag_step, 1)

            for k in range(UNITS):
                step(0, k, True, False)
            with dve.Fori(1, NORMS) as b:
                for k in range(UNITS):
                    step(b, k, False, False)
            for b in (NORMS, LAST):
                for k in range(UNITS):
                    step(b, k, False, b == LAST)
            divide(UNITS * B - 1, UNITS - 1)

            dve.wait_ge(x1_stored, 16 * B)

            def chunk_moments(c, t):
                dve.wait_ge(c_in, 16 * (c + 1))
                if t == 0:
                    dve.wait_ge(x_normed, ST * B)
                tile_moments(c_ln, t, ST * B + CT * c + t, t)

            def rows_low(c, m, slot):
                dve.wait_ge(c_hi_done, 2 * c + m + 1)
                dve.tensor_tensor(xt_lo[:, 2 * m:2 * m + 2, :], gu_ps[slot][:, :, :],
                                  xt_hi[:, 2 * m:2 * m + 2, :].bitcast(F32), ALU.subtract).then_inc(c_lo_done, 1)

            def hidden(c, i):
                n = IT * c + i
                slot = i % 2
                hs = i % HS
                dve.wait_ge(th_done, n + 1)
                dve.scalar_tensor_tensor(silu2[slot][:, :], th[slot][:, :], 1.0, gu_ps[slot][:, 0, :],
                                         ALU.add, ALU.mult).then_inc(silu_done, 1)
                dve.wait_ge(silu_done, n + 1)
                if i >= HS:
                    dve.wait_ge(hid_lo_done, n - HS + 1)
                dve.scalar_tensor_tensor(hid[hs][:, :], silu2[slot][:, :], hid_scale[:, i:i + 1], gu_ps[slot][:, 1, :],
                                         ALU.mult, ALU.mult).then_inc(hid_done, 1)

            def output(c):
                dve.wait_ge(down_done, IT * (c + 1))
                dve.wait_ge(cr_in, 16 * (c + 1))
                for t in range(CT):
                    dve.tensor_tensor(y_sb[:, t, :], acc_ps[t][:, :], down_gate[:, :], ALU.mult).then_inc(y_done, 1)

            def chunk(c, last):
                for i in range(IT):
                    hidden(c, i)
                    if not last and 3 <= i < 3 + CT:
                        chunk_moments(c + 1, i - 3)
                if not last:
                    rows_low(c + 1, 0, 1)
                    rows_low(c + 1, 1, 0)
                output(c)

            for t in range(CT):
                chunk_moments(0, t)
            rows_low(0, 0, 1)
            rows_low(0, 1, 0)
            with dve.Fori(0, NCH - 1) as c:
                chunk(c, False)
            chunk(NCH - 1, True)

        @block.scalar
        def _(act):
            act.wait_ge(gates_in, 32)
            act.activation(tgates[:, :], gates[:, :], ACT.Tanh).then_inc(tanh_done, 1)

            def queries_high(b, c, reused):
                act.wait_ge(qt_turned, 2 * b + c + 1)
                if reused:
                    act.wait_ge(qt_stored[c], 64 * b)
                act.activation(qt_hi[c][:, :, :], tr_ps[:, :].rearrange("p (j s) -> p j s", j=2),
                               ACT.Copy).then_inc(qt_hi_done, 1)

            def maxima_high(u, k):
                act.wait_ge(m_turned, u + 1)
                if not (isinstance(u, int) and u < 2):
                    act.wait_ge(m_in, 32 * (u - 1))
                act.activation(m_hi[k % 2][:, :], tr_ps[0:UH * ST, 0:P], ACT.Copy).then_inc(m_hi_done, 1)

            def exponents(u, j, reused):
                tt, i = divmod(j, PAIRS)
                act.wait_ge(t_done, 2 * PAIRS * u + j + 1)
                if i == 0 and reused:
                    act.wait_ge(pv_done, TT * (u - 1) + tt + 1)
                act.activation(probs[:, tt, i, :], t_ps[j % 2][:, :], ACT.Exp, scale=RSCALE).then_inc(exp_done, 1)

            def copy_output(u):
                act.wait_ge(pv_done, TT * (u + 1))
                act.activation(o_sb[:, :], o_ps[:, :], ACT.Copy).then_inc(o_copied, 1)

            for b in range(2):
                for c in range(2):
                    queries_high(b, c, b == 1)
            maxima_high(0, 0)

            def step(b, k, first, last):
                u = UNITS * b + k
                for j in range(2 * PAIRS):
                    exponents(u, j, not (first and k == 0))
                    if j == 1 and not (last and k == 3):
                        maxima_high(u + 1, k + 1)
                    if j == 3 and not (first and k == 0):
                        copy_output(u - 1)
                    if j == 4 and k >= 2 and not last and b is not NORMS:
                        queries_high(b + 2, k - 2, True)

            for k in range(UNITS):
                step(0, k, True, False)
            with act.Fori(1, NORMS) as b:
                for k in range(UNITS):
                    step(b, k, False, False)
            for b in (NORMS, LAST):
                for k in range(UNITS):
                    step(b, k, False, b == LAST)
            copy_output(UNITS * B - 1)

            def rows_high(c, m, slot):
                act.wait_ge(c_turned, 2 * c + m + 1)
                act.activation(xt_hi[:, 2 * m:2 * m + 2, :], gu_ps[slot][:, :, :], ACT.Copy).then_inc(c_hi_done, 1)

            def half_tanh(c, i):
                act.wait_ge(gu_done, IT * c + i + 1)
                act.activation(th[i % 2][:, :], gu_ps[i % 2][:, 0, :], ACT.Tanh,
                               scale=half_gs[:, i:i + 1]).then_inc(th_done, 1)

            def hidden_high(c, i):
                n = IT * c + i
                act.wait_ge(hid_done, n + 1)
                if i >= HS:
                    act.wait_ge(down_done, n - HS + 1)
                act.activation(hid_hi[i % HS][:, :], hid[i % HS][:, :], ACT.Copy).then_inc(hid_hi_done, 1)

            def chunk(c, last):
                for i in range(IT):
                    if i:
                        hidden_high(c, i - 1)
                    half_tanh(c, i)
                hidden_high(c, IT - 1)
                if not last:
                    rows_high(c + 1, 0, 1)
                    rows_high(c + 1, 1, 0)

            rows_high(0, 0, 1)
            rows_high(0, 1, 0)
            with act.Fori(0, NCH - 1) as c:
                chunk(c, False)
            chunk(NCH - 1, True)

        @block.tensor
        def _(pe):
            def turn_queries(b, c):
                pe.wait_ge(x_normed, ST * (b + 1))
                for j in range(2):
                    for st in range(ST):
                        at = j * S + st * P
                        mm = pe.transpose(tr_ps[:, at:at + P], x_norm[:, st, (2 * c + j) * P:(2 * c + j + 1) * P], ident[:, :])
                mm.then_inc(qt_turned, 1)

            def scores(b, k, j, reused):
                u = UNITS * b + k
                h, t = k // 2, j // 2
                if j == 0:
                    pe.wait_ge(q_in[k], 32 * (b + 1))
                    pe.wait_ge(k_max_done, 2 * b + h + 1)
                if j % 2 == 0 and reused:
                    pe.wait_ge(max_done, 4 * u + t - 1)
                for st in range(ST):
                    mm = pe.matmul(s_ps[t % 2][:, ST * (j % 2) + st, :], q_st[k][0:SROWS, j, st * P:(st + 1) * P],
                                   k_max[h][0:SROWS, kv_of(k, j // UG), :], start=True, stop=True)
                if j % 2:
                    mm.then_inc(s_done, 1)

            def turn_maxima(u, k):
                pe.wait_ge(max_done, 4 * (u + 1))
                pe.transpose(tr_ps[0:UH * ST, 0:P], negmax[k % 2][:, :], ident[:, :]).then_inc(m_turned, 1)

            def shifted(b, k, j, reused):
                u = UNITS * b + k
                h = k // 2
                tt, i = divmod(j, PAIRS)
                if j == 0:
                    pe.wait_ge(m_in, 32 * (u + 1))
                    pe.wait_ge(k_exp_done, 2 * b + h + 1)
                if reused:
                    pe.wait_ge(exp_done, 2 * PAIRS * u + j - 1)
                pe.matmul(t_ps[j % 2][:, :], k_exp[h][0:DROWS, kv_of(k, i), tt * P:(tt + 1) * P],
                          q_st[k][0:DROWS, UG * i:UG * i + UG, :].rearrange("p g s -> p (g s)"),
                          start=True, stop=True).then_inc(t_done, 1)

            def weigh(b, k, tt, reused):
                u = UNITS * b + k
                h = k // 2
                pe.wait_ge(exp_done, 2 * PAIRS * u + PAIRS * (tt + 1))
                if tt == 0:
                    pe.wait_ge(v_done, TT * (2 * b + h + 1))
                    if reused:
                        pe.wait_ge(o_copied, u)
                for i in range(PAIRS):
                    mm = pe.matmul(o_ps[i * VW:(i + 1) * VW, :], v_aug[h][:, tt, kv_of(k, i), :], probs[:, tt, i, :],
                                   start=(tt == 0), stop=(tt == TT - 1))
                mm.then_inc(pv_done, 1)

            def turn_output(u):
                pe.wait_ge(o_copied, u + 1)
                for j in range(UG * ST):
                    mm = pe.transpose(tr_ps[:, j * P:(j + 1) * P], o_sb[:, j * P:(j + 1) * P], ident[:, :])
                mm.then_inc(o_turned, 1)

            pe.wait_ge(ident_done, 1)
            turn_queries(0, 0)
            pe.wait_ge(qt_lo_done, 1)
            turn_queries(0, 1)
            pe.wait_ge(qt_lo_done, 2)
            turn_queries(1, 0)
            pe.wait_ge(qt_lo_done, 3)
            turn_queries(1, 1)
            for k in range(2):
                for j in range(UH):
                    scores(0, k, j, k > 0 or j >= 4)
                if k == 1:
                    pe.wait_ge(qt_lo_done, 4)
                    turn_maxima(0, 0)

            def step(b, k, first, last):
                u = UNITS * b + k
                norming = not last and b is not NORMS
                ahead = (b, k + 2) if k < 2 else (b + 1, k - 2)
                started = not (first and k == 0)
                for j in range(UH):
                    shifted(b, k, j, started or j >= 2)
                    if not (last and k >= 2):
                        scores(*ahead, j, True)
                    if j == 1 and not (last and k == 3):
                        if first and k < 2:
                            pe.wait_ge(m_lo_done, k + 1)
                        else:
                            pe.wait_ge(o_normed, u - 1)
                        turn_maxima(u + 1, k + 1)
                    if j == 2 and started:
                        weigh(*((b, k - 1) if k else (b - 1, UNITS - 1)), 1, True)
                    if j == 3 and norming and k >= 2:
                        pe.wait_ge(m_lo_done, u + 2)
                        turn_queries(b + 2, k - 2)
                    if j == 3 and b is NORMS and k == 2:
                        pe.wait_ge(m_lo_done, u + 2)
                        pe.wait_ge(flag_step, 2)
                        pe.transpose(tr_ps[0:1, 0:P], low_col[:, :], ident[:, :]).then_inc(flag_turned, 1)
                    if j == 5 and started:
                        if norming and k >= 2:
                            pe.wait_ge(qt_lo_done, 2 * (b + 2) + k - 1)
                        elif b is NORMS and k == 2:
                            pe.wait_ge(flag_done, 1)
                        elif last and k == 3:
                            pe.wait_ge(o_normed, u - 1)
                        else:
                            pe.wait_ge(m_lo_done, u + 2)
                        turn_output(u - 1)
                    if j == 6:
                        weigh(b, k, 0, started)

            for k in range(UNITS):
                step(0, k, True, False)
            with pe.Fori(1, NORMS) as b:
                for k in range(UNITS):
                    step(b, k, False, False)
            for b in (NORMS, LAST):
                for k in range(UNITS):
                    step(b, k, False, b == LAST)
            weigh(LAST, UNITS - 1, 1, True)
            pe.wait_ge(o_normed, UNITS * B - 1)
            turn_output(UNITS * B - 1)

            TURNS = IT + 2

            def free_slots(c, used):
                if used <= 2:
                    pe.wait_ge(c_lo_done, 2 * c + used)
                else:
                    pe.wait_ge(hid_done, IT * c + used - 2)

            def turn_rows(c, m, slot):
                pe.wait_ge(c_normed, CT * (c + 1))
                for kk in range(2):
                    for t in range(CT):
                        k = 2 * m + kk
                        mm = pe.transpose(gu_ps[slot][:, kk, t * P:(t + 1) * P], c_norm[:, t, k * P:(k + 1) * P],
                                          ident[:, :])
                mm.then_inc(c_turned, 1)

            def feed_forward(kind):
                def as_kind(ap):
                    return ap if kind == F32R else ap.bitcast(kind)

                def gate_up(c, i):
                    slot = i % 2
                    free_slots(c, 2 if i == 0 else i + 1)
                    for half, w in ((0, gate_w), (1, up_w)):
                        for k in range(KT):
                            for part in (xt_hi, xt_lo):
                                mm = pe.matmul(gu_ps[slot][:, half, :], as_kind(w[:, k, i * P:(i + 1) * P]),
                                               as_kind(part[:, k, :]), start=(k == 0 and part is xt_hi),
                                               stop=(k == KT - 1 and part is xt_lo))
                    mm.then_inc(gu_done, 1)

                def down(c, i):
                    pe.wait_ge(hid_lo_done, IT * c + i + 1)
                    for t in range(CT):
                        for part in (hid_hi, hid_lo):
                            mm = pe.matmul(acc_ps[t][:, :], as_kind(part[i % HS][:, t * P:(t + 1) * P]),
                                           as_kind(down_w[:, i, :]), start=(i == 0 and part is hid_hi),
                                           stop=(i == IT - 1 and part is hid_lo))
                    mm.then_inc(down_done, 1)

                def chunk(c, last):
                    for i in range(IT - 1):
                        gate_up(c, i)
                        if i >= LAG:
                            down(c, i - LAG)
                    gate_up(c, IT - 1)
                    down(c, IT - 3)
                    if not last:
                        free_slots(c, IT + 1)
                        turn_rows(c + 1, 0, 1)
                        free_slots(c, IT + 2)
                        turn_rows(c + 1, 1, 0)
                    down(c, IT - 2)
                    down(c, IT - 1)

                with pe.Fori(0, NCH - 1) as c:
                    chunk(c, False)
                chunk(NCH - 1, True)

            pe.wait_ge(o_normed, UNITS * B)
            turn_rows(0, 0, 1)
            turn_rows(0, 1, 0)
            pe.wait_ge(w_set, 16 * WPIECES)
            pe.wait_ge(flag_done, 1)
            inexact = pe.value_load(low_flag[0:1, 0:1])
            with pe.If(inexact == 0):
                feed_forward(F32R)
            with pe.Else():
                feed_forward(F32)


_INS = ["x", "ctx_n", "ctx_t", "g_xattn", "g_ffn", "weights", "gate_s", "up_s", "down_s"]


def kernel(x, ctx_512, g_xattn, g_ffn, L0_ffn_gate_w, L0_ffn_up_w, L0_ffn_down_w, L0_ffn_gate_s, L0_ffn_up_s,
           L0_ffn_down_s):
    import concourse.bacc as bacc
    from concourse.bass_utils import run_bass_kernel_spmd

    def rows_on_partitions(w):
        n = w.shape[0] // P
        return w.reshape(n, P, w.shape[1]).transpose(1, 0, 2).reshape(P, -1)

    ctx = np.asarray(ctx_512)
    arrays = {
        "x": np.asarray(x), "ctx_n": ctx, "ctx_t": ctx.reshape(B * T, KV * D).T,
        "g_xattn": np.asarray(g_xattn), "g_ffn": np.asarray(g_ffn),
        "weights": np.concatenate([rows_on_partitions(np.asarray(w).T)
                                   for w in (L0_ffn_gate_w, L0_ffn_up_w, L0_ffn_down_w)], axis=1),
        "gate_s": np.asarray(L0_ffn_gate_s).reshape(IT, P).T, "up_s": np.asarray(L0_ffn_up_s).reshape(IT, P).T,
        "down_s": np.asarray(L0_ffn_down_s),
    }
    nc = bacc.Bacc("TRN2", target_bir_lowering=False, num_devices=1)
    args = []
    for name in _INS:
        arrays[name] = np.ascontiguousarray(arrays[name])
        args.append(nc.dram_tensor(name, arrays[name].shape, F32, kind="ExternalInput").ap())
    out = nc.dram_tensor("out", [B, S, E], F32, kind="ExternalOutput").ap()
    build(nc, *args, out)
    r = run_bass_kernel_spmd(nc, [arrays], core_ids=[0])
    return r.results[0]["out"]
```

```python
import numpy as np
import concourse.bass as bass
from concourse import mybir
from contextlib import ExitStack

F32 = mybir.dt.float32
F32R = mybir.dt.float32r
I32 = mybir.dt.int32
ALU = mybir.AluOpType
ACT = mybir.ActivationFunctionType
AX = mybir.AxisListType

P = 128
B, S, E = 8, 256, 512
T = 256
H, KV, D = 32, 8, 16
G = H // KV
ST = S // P
TT = T // P
UNITS = 4
PAIRS, UG = 4, 2
UH = PAIRS * UG
UKV = KV // 2
NPART = 4
ZROW = NPART * D
HIROW, LOROW = ZROW + 1, ZROW + 2
SROWS, DROWS = ZROW + 1, ZROW + 3
VW = 32
F = 1408
IT = F // P
KT = E // P
CH = 512
CT = CH // P
NCH = B * S // CH
HS = 3
LAG = 2
WCOLS = 3 * KT * F
WPIECES = 6
WP = WCOLS // WPIECES
WQ = WP // UNITS
EPS = 1e-5
LOW_BITS = 0xFFF
RSCALE = 1.0 / float(D) ** 0.5


def kv_of(k, pair):
    return (k % 2) * 2 + pair // 2


def build(nc, x, ctx_n, ctx_t, g_xattn, g_ffn, weights, gate_s, up_s, down_s, out):
    q_parts = nc.dram_tensor("q_parts", [B, UNITS, UH, 2, D, S], F32).ap()
    x1_dram = nc.dram_tensor("x1_scratch", [B * S, E], F32).ap()

    with ExitStack() as top:
        def sem(name):
            return top.enter_context(nc.semaphore(name))

        def sb(stack, name, shape, dt=F32):
            return stack.enter_context(nc.sbuf_tensor(name, shape, dt))

        def ps(stack, name, shape, dt=F32):
            return stack.enter_context(nc.psum_tensor(name, shape, dt))

        w_sb = sb(top, "w_sb", [P, WCOLS], F32R)
        ident = sb(top, "ident", [P, P])
        ident_zero = sb(top, "ident_zero", [P, P])
        gates = sb(top, "gates", [P, 2])
        tgates = sb(top, "tgates", [P, 2])
        gs_col = sb(top, "gs_col", [P, IT])
        us_col = sb(top, "us_col", [P, IT])
        half_gs = sb(top, "half_gs", [P, IT])
        hid_scale = sb(top, "hid_scale", [P, IT])
        down_row = sb(top, "down_row", [P, E])
        down_gate = sb(top, "down_gate", [P, E])
        bits = sb(top, "bits", [P, WQ], I32)
        low_bits = sb(top, "low_bits", [P, WQ], I32)
        low_col = sb(top, "low_col", [P, 1])
        low_flag = sb(top, "low_flag", [1, 1], I32)
        minus_half = sb(top, "minus_half", [P, CT])
        stats = sb(top, "stats", [P, CT, 6])
        moments = sb(top, "moments", [P, CT, 2])
        var_eps = sb(top, "var_eps", [P, CT])
        rstd = sb(top, "rstd", [P, CT])
        mean_rstd = sb(top, "mean_rstd", [P, CT])
        shift = sb(top, "shift", [P, CT])

        attn = sb(top, "attn", [P, ST, E])
        x_res = sb(top, "x_res", [P, ST, E])

        att = ExitStack()
        w_stage = sb(att, "w_stage", [P, WP])
        x_ln = sb(att, "x_ln", [P, ST, E])
        x_norm = sb(att, "x_norm", [P, ST, E])
        k_raw = sb(att, "k_raw", [ZROW, KV, T])
        qt = sb(att, "qt", [P, 2, S])
        qt_hi = [sb(att, f"qt_hi{h}", [P, 2, S], F32R) for h in range(2)]
        qt_lo = [sb(att, f"qt_lo{h}", [P, 2, S], F32R) for h in range(2)]
        q_st = [sb(att, f"q_st{k}", [DROWS, UH, S], F32R) for k in range(UNITS)]
        k_max = [sb(att, f"k_max{h}", [DROWS, UKV, T], F32R) for h in range(2)]
        k_exp = [sb(att, f"k_exp{h}", [DROWS, UKV, T], F32R) for h in range(2)]
        v_raw = sb(att, "v_raw", [P, TT, KV * D])
        v_aug = [sb(att, f"v_aug{h}", [P, TT, UKV, VW]) for h in range(2)]
        probs = sb(att, "probs", [P, TT, PAIRS, UG * S])
        o_sb = sb(att, "o_sb", [P, UG * S])
        rden = sb(att, "rden", [P, UG * ST, PAIRS])
        negmax = [sb(att, f"negmax{h}", [P, UH * ST]) for h in range(2)]
        m_parts = [sb(att, f"m_parts{h}", [P, 2, UH * ST], F32R) for h in range(2)]
        m_rows = [sb(att, f"m_rows{h}", [2 * UH * ST, P]) for h in range(2)]
        s_ps = [ps(att, f"s_ps{h}", [P, 2 * ST, T]) for h in range(2)]
        t_ps = [ps(att, f"t_ps{h}", [P, UG * S]) for h in range(2)]
        o_ps = ps(att, "o_ps", [P, UG * S])
        tr_ps = ps(att, "tr_ps", [P, 2 * S])
        att.close()

        ffn = ExitStack()
        c_ln = sb(ffn, "c_ln", [P, CT, E])
        c_norm = sb(ffn, "c_norm", [P, CT, E])
        xt_hi = sb(ffn, "xt_hi", [P, KT, CH], F32R)
        xt_lo = sb(ffn, "xt_lo", [P, KT, CH], F32R)
        c_res = sb(ffn, "c_res", [P, CT, E])
        th = [sb(ffn, f"th{h}", [P, CH]) for h in range(2)]
        silu2 = [sb(ffn, f"silu2{h}", [P, CH]) for h in range(2)]
        hid = [sb(ffn, f"hid{h}", [P, CH]) for h in range(HS)]
        hid_hi = [sb(ffn, f"hid_hi{h}", [P, CH], F32R) for h in range(HS)]
        hid_lo = [sb(ffn, f"hid_lo{h}", [P, CH], F32R) for h in range(HS)]
        y_sb = sb(ffn, "y_sb", [P, CT, E])
        gu_ps = [ps(ffn, f"gu_ps{h}", [P, 2, CH]) for h in range(2)]
        acc_ps = [ps(ffn, f"acc_ps{t}", [P, E]) for t in range(CT)]
        ffn.close()

        gates_in = sem("gates_in")
        scales_in = sem("scales_in")
        filled = sem("filled")
        padded = sem("padded")
        ident_done = sem("ident_done")
        tanh_done = sem("tanh_done")
        scales_done = sem("scales_done")
        x_in = sem("x_in")
        stat_done = sem("stat_done")
        moments_done = sem("moments_done")
        norm_chain = sem("norm_chain")
        x_normed = sem("x_normed")
        qt_turned = sem("qt_turned")
        qt_copied = sem("qt_copied")
        qt_hi_done = sem("qt_hi_done")
        qt_lo_done = sem("qt_lo_done")
        qt_stored = [sem(f"qt_stored{h}") for h in range(2)]
        q_in = [sem(f"q_in{k}") for k in range(UNITS)]
        k_in = sem("k_in")
        k_hi_done = sem("k_hi_done")
        k_max_done = sem("k_max_done")
        k_exp_done = sem("k_exp_done")
        v_in = sem("v_in")
        v_done = sem("v_done")
        s_done = sem("s_done")
        max_done = sem("max_done")
        m_hi_done = sem("m_hi_done")
        m_lo_done = sem("m_lo_done")
        m_turned = sem("m_turned")
        m_copied = sem("m_copied")
        m_in = sem("m_in")
        t_done = sem("t_done")
        exp_done = sem("exp_done")
        pv_done = sem("pv_done")
        o_copied = sem("o_copied")
        o_turned = sem("o_turned")
        rden_done = sem("rden_done")
        o_normed = sem("o_normed")
        r_in = sem("r_in")
        gated_done = sem("gated_done")
        x1_done = sem("x1_done")
        x1_stored = sem("x1_stored")
        w_in = sem("w_in")
        w_seen = sem("w_seen")
        w_set = sem("w_set")
        flag_step = sem("flag_step")
        flag_turned = sem("flag_turned")
        flag_done = sem("flag_done")
        c_in = sem("c_in")
        c_normed = sem("c_normed")
        c_turned = sem("c_turned")
        c_hi_done = sem("c_hi_done")
        c_lo_done = sem("c_lo_done")
        gu_done = sem("gu_done")
        th_done = sem("th_done")
        silu_done = sem("silu_done")
        hid_done = sem("hid_done")
        hid_hi_done = sem("hid_hi_done")
        hid_lo_done = sem("hid_lo_done")
        down_done = sem("down_done")
        acc_done = sem("acc_done")
        y_done = sem("y_done")
        cr_in = sem("cr_in")
        out_ready = sem("out_ready")
        out_stored = sem("out_stored")

        sp_passed, pool_passed, dve_passed = sem("sp_passed"), sem("pool_passed"), sem("dve_passed")

        block = top.enter_context(nc.Block())

        kt_view = ctx_t.rearrange("(v d) (b t) -> b d v t", d=D, b=B)
        v_view = ctx_n.rearrange("b (tt p) e -> b p tt e", p=P)
        x_view = x.rearrange("b (st p) e -> b p st e", p=P)
        x1w_view = x1_dram.rearrange("(b st p) e -> b p st e", p=P, st=ST)
        x1c_view = x1_dram.rearrange("(c ct p) e -> c p ct e", p=P, ct=CT)
        out_view = out.rearrange("b s e -> (b s) e").rearrange("(c ct p) e -> c p ct e", p=P, ct=CT)
        gate_w = w_sb[:, 0:KT * F].rearrange("p (k i) -> p k i", k=KT)
        up_w = w_sb[:, KT * F:2 * KT * F].rearrange("p (k i) -> p k i", k=KT)
        down_w = w_sb[:, 2 * KT * F:WCOLS].rearrange("p (i h) -> p i h", i=IT)
        attn_units = attn[:, :, :].rearrange("p st (k i g d) -> p k g st i d", k=UNITS, i=PAIRS, g=UG)

        def waited(engine, passed):
            engine.sem_inc(passed)

        LAST = B - 1
        NORMS = B - 2

        @block.sync
        def _(sp):
            def load_x(b):
                sp.dma_start(x_ln[:, :, :], x_view[b]).then_inc(x_in, 16)

            def load_k(b):
                for r in range(NPART):
                    sp.dma_start(k_raw[r * D:(r + 1) * D, :, :], kt_view[b]).then_inc(k_in, 16)

            def load_v(b):
                sp.dma_start(v_raw[:, :, :], v_view[b]).then_inc(v_in, 16)

            def store_q(b, c):
                sp.wait_ge(qt_lo_done, 2 * b + c + 1)
                for part, tile in ((0, qt_hi[c]), (1, qt_lo[c])):
                    for j in range(2):
                        sp.dma_start(q_parts[b, 2 * c + j, :, part, :, :], tile[:, j, :].bitcast(F32)).then_inc(qt_stored[c], 16)

            def load_q(b, k, reused):
                sp.wait_ge(qt_stored[k // 2], 64 * (b + 1))
                if reused:
                    waited(sp, sp_passed)
                    sp.wait_ge(t_done, 2 * PAIRS * (UNITS * (b - 1) + k + 1))
                waited(sp, sp_passed)
                src = q_parts[b, k].rearrange("h part d s -> (part d) h s")
                for r in range(2):
                    sp.dma_start(q_st[k][r * 2 * D:(r + 1) * 2 * D, :, :].bitcast(F32), src).then_inc(q_in[k], 16)

            def place_maxima(b, k):
                sp.wait_ge(m_copied, UNITS * b + k + 1)
                sp.dma_start(q_st[k][HIROW:LOROW + 1, :, :].bitcast(F32), m_rows[k % 2][:, :]).then_inc(m_in, 16)

            load_x(0)
            sp.dma_start(gates[:, 0:1], g_xattn.partition_broadcast(P)).then_inc(gates_in, 16)
            sp.dma_start(gates[:, 1:2], g_ffn.partition_broadcast(P)).then_inc(gates_in, 16)
            load_k(0)
            load_v(0)
            sp.wait_ge(x_normed, ST)
            load_x(1)
            for c in range(2):
                store_q(0, c)
            for k in range(3):
                load_q(0, k, False)
            sp.wait_ge(x_normed, 2 * ST)
            load_x(2)
            sp.wait_ge(k_max_done, 2)
            load_k(1)
            for c in range(2):
                store_q(1, c)
            sp.dma_start(gs_col[:, :], gate_s).then_inc(scales_in, 16)
            sp.dma_start(us_col[:, :], up_s).then_inc(scales_in, 16)
            sp.dma_start(down_row[:, :], down_s.partition_broadcast(P)).then_inc(scales_in, 16)
            place_maxima(0, 0)

            def step(b, k, first, last):
                norming = not last and b is not NORMS
                if k == 0:
                    load_q(b, 3, not first)
                elif not last:
                    load_q(b + 1, k - 1, True)
                if k < 3:
                    place_maxima(b, k + 1)
                elif not last:
                    place_maxima(b + 1, 0)
                if k == 2 and not last:
                    sp.wait_ge(v_done, 2 * TT * (b + 1))
                    load_v(b + 1)
                if k == 1:
                    if not first:
                        sp.wait_ge(x1_done, b)
                        sp.dma_start(x1w_view[b - 1], x_res[:, :, :]).then_inc(x1_stored, 16)
                        sp.wait_ge(x1_stored, 16 * b)
                    sp.dma_start(x_res[:, :, :], x_view[b]).then_inc(r_in, 16)
                if k == 2 and norming:
                    sp.wait_ge(k_max_done, 2 * (b + 2))
                    load_k(b + 2)
                if norming:
                    if k == 0:
                        if not first:
                            sp.wait_ge(w_set, 16 * b)
                            sp.wait_ge(w_seen, UNITS * b)
                        sp.dma_start(w_stage[:, :], weights[:, bass.ds(b * WP, WP)]).then_inc(w_in, 16)
                    if k == 1:
                        sp.wait_ge(w_in, 16 * (b + 1))
                        waited(sp, sp_passed)
                        sp.dma_start(w_sb[:, bass.ds(b * WP, WP)].bitcast(F32), w_stage[:, :]).then_inc(w_set, 16)
                if k == 3 and norming:
                    store_q(b + 2, 0)
                if k == 0 and not first and not last:
                    store_q(b + 1, 1)

            def next_x(b, k):
                if k == 2:
                    sp.wait_ge(x_normed, ST * (b + 3))
                    load_x(b + 3)

            for k in range(UNITS):
                step(0, k, True, False)
                next_x(0, k)
            with sp.Fori(1, NORMS - 1) as b:
                for k in range(UNITS):
                    step(b, k, False, False)
                    next_x(b, k)
            for b in (NORMS - 1, NORMS):
                for k in range(UNITS):
                    step(b, k, False, False)
            sp.wait_ge(w_seen, UNITS * WPIECES)
            sp.wait_ge(w_set, 16 * WPIECES)
            sp.wait_ge(x_normed, ST * B)
            sp.dma_start(c_ln[:, :, :], x1c_view[0]).then_inc(c_in, 16)
            for k in range(UNITS):
                step(LAST, k, False, True)
            sp.wait_ge(x1_done, B)
            sp.dma_start(x1w_view[LAST], x_res[:, :, :]).then_inc(x1_stored, 16)

            sp.wait_ge(x1_stored, 16 * B)

            def load_chunk(c):
                sp.dma_start(c_ln[:, :, :], x1c_view[c]).then_inc(c_in, 16)

            def load_residual(c):
                sp.dma_start(c_res[:, :, :], x1c_view[c]).then_inc(cr_in, 16)

            def store_out(c):
                for t in range(CT):
                    sp.wait_ge(out_ready, CT * c + t + 1)
                    sp.dma_start(out_view[c, :, t, :], y_sb[:, t, :]).then_inc(out_stored, 16)

            load_residual(0)
            with sp.Fori(0, NCH - 1) as c:
                sp.wait_ge(c_normed, CT * (c + 1))
                load_chunk(c + 1)
                store_out(c)
                sp.wait_ge(out_stored, 16 * CT * (c + 1))
                load_residual(c + 1)
            store_out(NCH - 1)
            sp.wait_ge(out_stored, 16 * CT * NCH)

        @block.gpsimd
        def _(pool):
            pool.memset(ident_zero[:, :], 0.0).then_inc(filled, 1)
            pool.wait_ge(filled, 1)
            pool.affine_select(out=ident[:, :], in_=ident_zero[:, :], compare_op=ALU.not_equal, fill=1.0, base=0,
                               pattern=[[-1, P]], channel_multiplier=1).then_inc(ident_done, 1)
            pool.memset(minus_half[:, :], -0.5).then_inc(filled, 1)

            def norm_tiles(rows, n, src, dst, tiles, done):
                pool.wait_ge(moments_done, tiles)
                waited(pool, pool_passed)
                pool.tensor_scalar(var_eps[:, 0:n], moments[:, 0:n, 1], 1.0, EPS, ALU.mult, ALU.add).then_inc(norm_chain, 1)
                pool.wait_ge(norm_chain, 4 * rows + 1)
                pool.tensor_tensor(rstd[:, 0:n], var_eps[:, 0:n], minus_half[:, 0:n], ALU.pow).then_inc(norm_chain, 1)
                pool.wait_ge(norm_chain, 4 * rows + 2)
                pool.tensor_tensor(mean_rstd[:, 0:n], moments[:, 0:n, 0], rstd[:, 0:n], ALU.mult).then_inc(norm_chain, 1)
                pool.wait_ge(norm_chain, 4 * rows + 3)
                waited(pool, pool_passed)
                pool.tensor_scalar(shift[:, 0:n], mean_rstd[:, 0:n], -1.0, 0.0, ALU.mult, ALU.add).then_inc(norm_chain, 1)
                pool.wait_ge(norm_chain, 4 * rows + 4)
                waited(pool, pool_passed)
                for t in range(n):
                    pool.tensor_scalar(dst[:, t, :], src[:, t, :], rstd[:, t:t + 1], shift[:, t:t + 1],
                                       ALU.mult, ALU.add).then_inc(done, 1)

            def norm_batch(b, reused):
                if reused:
                    pool.wait_ge(qt_turned, 2 * b)
                norm_tiles(b, ST, x_ln, x_norm, ST * (b + 1), x_normed)

            def queries_low(b, c, reused):
                pool.wait_ge(qt_hi_done, 2 * b + c + 1)
                if reused:
                    pool.wait_ge(qt_stored[c], 64 * b)
                pool.tensor_tensor(qt_lo[c][:, :, :], qt[:, :, :], qt_hi[c][:, :, :].bitcast(F32),
                                   ALU.subtract).then_inc(qt_lo_done, 1)

            def keys_for_max(b, h, reused):
                n = 2 * b + h
                pool.wait_ge(k_in, 16 * NPART * (b + 1))
                if reused:
                    pool.wait_ge(s_done, PAIRS * (UNITS * (b - 1) + 2 * h + 2))
                    pool.wait_ge(k_exp_done, 2 * (b - 1) + h + 1)
                waited(pool, pool_passed)
                raw = k_raw[:, h * UKV:(h + 1) * UKV, :]
                half = slice(ZROW // 2, ZROW)
                pool.tensor_scalar(k_max[h][0:ZROW, :, :], raw, 1.0, 0.0, ALU.mult, ALU.add).then_inc(k_hi_done, 1)
                pool.wait_ge(k_hi_done, n + 1)
                pool.tensor_tensor(k_max[h][half, :, :], raw[half, :, :],
                                   k_max[h][half, :, :].bitcast(F32), ALU.subtract).then_inc(k_max_done, 1)
                pool.wait_ge(k_max_done, n + 1)

            def keys_for_exp(b, h, reused):
                pool.wait_ge(k_max_done, 2 * b + h + 1)
                if reused:
                    pool.wait_ge(t_done, 2 * PAIRS * (UNITS * (b - 1) + 2 * h + 2))
                waited(pool, pool_passed)
                pool.tensor_scalar(k_exp[h][0:ZROW, :, :], k_max[h][0:ZROW, :, :].bitcast(F32), 1.0, 0.0,
                                   ALU.mult, ALU.add).then_inc(k_exp_done, 1)

            def values(b, h, reused):
                pool.wait_ge(v_in, 16 * (b + 1))
                if reused:
                    pool.wait_ge(pv_done, TT * (UNITS * (b - 1) + 2 * h + 2))
                waited(pool, pool_passed)
                for tt in range(TT):
                    src = v_raw[:, tt, h * UKV * D:(h + 1) * UKV * D].rearrange("p (v d) -> p v d", d=D)
                    pool.tensor_scalar(v_aug[h][:, tt, :, 0:D], src, 1.0, 0.0, ALU.mult, ALU.add).then_inc(v_done, 1)

            def residual(b):
                pool.wait_ge(o_normed, UNITS * (b + 1))
                waited(pool, pool_passed)
                pool.tensor_scalar(attn[:, :, :], attn[:, :, :], tgates[:, 0:1], 0.0,
                                   ALU.mult, ALU.add).then_inc(gated_done, 1)
                pool.wait_ge(gated_done, b + 1)
                pool.wait_ge(r_in, 16 * (b + 1))
                pool.tensor_tensor(x_res[:, :, :], x_res[:, :, :], attn[:, :, :], ALU.add).then_inc(x1_done, 1)

            pool.wait_ge(filled, 2)
            norm_batch(0, False)
            for c in range(2):
                queries_low(0, c, False)
            keys_for_max(0, 0, False)
            norm_batch(1, True)
            keys_for_exp(0, 0, False)
            for c in range(2):
                queries_low(1, c, True)
            keys_for_max(0, 1, False)
            keys_for_exp(0, 1, False)
            for h in range(2):
                values(0, h, False)
            pool.wait_ge(tanh_done, 1)

            def step(b, k, first, last):
                if k == 3 and not last and b is not NORMS:
                    queries_low(b + 2, 0, True)
                if k == 0:
                    if not first and not last:
                        queries_low(b + 1, 1, True)
                    if not last:
                        keys_for_max(b + 1, 0, True)
                    if not first:
                        keys_for_exp(b, 1, True)
                        residual(b - 1)
                if k == 1:
                    if not first:
                        values(b, 1, True)
                    if not last and b is not NORMS:
                        norm_batch(b + 2, True)
                if k == 2 and not last:
                    keys_for_max(b + 1, 1, True)
                    keys_for_exp(b + 1, 0, True)
                if k == 3 and not last:
                    values(b + 1, 0, True)

            for k in range(UNITS):
                step(0, k, True, False)
            with pool.Fori(1, NORMS) as b:
                for k in range(UNITS):
                    step(b, k, False, False)
            def norm_chunk(c, reused):
                pool.wait_ge(c_in, 16 * (c + 1))
                if reused:
                    pool.wait_ge(c_turned, 2 * c)
                else:
                    pool.wait_ge(qt_turned, 2 * B)
                norm_tiles(B + c, CT, c_ln, c_norm, ST * B + CT * (c + 1), c_normed)

            def hidden_low(n, slot):
                pool.wait_ge(hid_hi_done, n + 1)
                pool.tensor_tensor(hid_lo[slot][:, :], hid[slot][:, :], hid_hi[slot][:, :].bitcast(F32),
                                   ALU.subtract).then_inc(hid_lo_done, 1)

            def add_residual(c, t):
                pool.wait_ge(y_done, CT * c + t + 1)
                pool.wait_ge(cr_in, 16 * (c + 1))
                pool.tensor_tensor(y_sb[:, t, :], y_sb[:, t, :], c_res[:, t, :], ALU.add).then_inc(out_ready, 1)

            def chunk(c, last):
                for i in range(2, IT):
                    hidden_low(IT * c + i, i % HS)
                    if i == 7 and not last:
                        norm_chunk(c + 1, True)
                if last:
                    for t in range(CT):
                        add_residual(c, t)
                else:
                    add_residual(c, 0)
                    add_residual(c, 1)
                    hidden_low(IT * (c + 1), 0)
                    add_residual(c, 2)
                    hidden_low(IT * (c + 1) + 1, 1)
                    add_residual(c, 3)

            for b in (NORMS, LAST):
                for k in range(UNITS):
                    step(b, k, False, b == LAST)
                    if b == LAST and k == 1:
                        norm_chunk(0, False)
            residual(LAST)

            hidden_low(0, 0)
            hidden_low(1, 1)
            with pool.Fori(0, NCH - 1) as c:
                chunk(c, False)
            chunk(NCH - 1, True)

        @block.vector
        def _(dve):
            def tile_moments(src, t, n, col):
                dve.bn_stats(stats[:, t, :], src[:, t, :]).then_inc(stat_done, 1)
                dve.wait_ge(stat_done, n + 1)
                waited(dve, dve_passed)
                dve.bn_aggr(moments[:, t, :], stats[:, t, :]).then_inc(moments_done, 1)

            def batch_moments(b, t, reused):
                dve.wait_ge(x_in, 16 * (b + 1))
                if reused:
                    dve.wait_ge(x_normed, ST * b)
                tile_moments(x_ln, t, ST * b + t, t)

            def maxima(b, k, t, reused):
                u = UNITS * b + k
                dve.wait_ge(s_done, PAIRS * u + t + 1)
                if t == 0 and reused:
                    dve.wait_ge(m_lo_done, u - 1)
                dve.tensor_reduce(negmax[k % 2][:, 4 * t:4 * t + 4], s_ps[t % 2][:, :, :], AX.X, ALU.max,
                                  negate=True).then_inc(max_done, 1)

            def split_maxima(u, k, reused):
                parts = m_parts[k % 2]
                dve.wait_ge(max_done, 4 * (u + 1))
                if reused:
                    dve.wait_ge(m_turned, u - 1)
                waited(dve, dve_passed)
                dve.tensor_copy(parts[:, 0, :], negmax[k % 2][:, :]).then_inc(m_hi_done, 1)
                dve.wait_ge(m_hi_done, u + 1)
                dve.tensor_tensor(parts[:, 1, :], negmax[k % 2][:, :], parts[:, 0, :].bitcast(F32),
                                  ALU.subtract).then_inc(m_lo_done, 1)

            def divide(u, k):
                dve.wait_ge(o_turned, u + 1)
                turned = tr_ps[:, :].rearrange("p (j i w) -> p j i w", j=UG * ST, i=PAIRS)
                dve.reciprocal(rden[:, :, :], turned[:, :, :, D]).then_inc(rden_done, 1)
                dve.wait_ge(rden_done, u + 1)
                for g in range(UG):
                    mul = dve.tensor_tensor(attn_units[:, k, g], turned[:, ST * g:ST * g + ST, :, 0:D],
                                            rden[:, ST * g:ST * g + ST, :].unsqueeze(3).broadcast_to([P, ST, PAIRS, D]),
                                            ALU.mult)
                mul.then_inc(o_normed, 1)

            for t in range(ST):
                batch_moments(0, t, False)
            for k in range(UNITS):
                dve.memset(q_st[k][ZROW:SROWS, :, :].bitcast(F32), 0.0).then_inc(padded, 1)
            for h in range(2):
                dve.memset(k_max[h][ZROW:DROWS, :, :].bitcast(F32), 1.0).then_inc(padded, 1)
                dve.memset(k_exp[h][ZROW:DROWS, :, :].bitcast(F32), 1.0).then_inc(padded, 1)
                dve.memset(v_aug[h][:, :, :, D + 1:VW], 0.0).then_inc(padded, 1)
                dve.memset(v_aug[h][:, :, :, D:D + 1], 1.0).then_inc(padded, 1)

            dve.memset(bits[:, :], 0).then_inc(padded, 1)

            for t in range(ST):
                batch_moments(1, t, t == 0)
            for k in range(2):
                for t in range(4):
                    maxima(0, k, t, False)
                split_maxima(k, k, False)
            dve.wait_ge(padded, UNITS + 9)
            dve.wait_ge(scales_in, 48)
            dve.tensor_scalar(half_gs[:, :], gs_col[:, :], 0.5, None, ALU.mult).then_inc(scales_done, 1)
            dve.wait_ge(scales_done, 1)
            dve.tensor_tensor(hid_scale[:, :], half_gs[:, :], us_col[:, :], ALU.mult).then_inc(scales_done, 1)
            dve.wait_ge(tanh_done, 1)
            dve.tensor_scalar(down_gate[:, :], down_row[:, :], tgates[:, 1:2], None, ALU.mult).then_inc(scales_done, 1)

            def step(b, k, first, last):
                u = UNITS * b + k
                norming = not last and b is not NORMS
                ahead = (b, k + 2) if k < 2 else (b + 1, k - 2)
                for t in range(4):
                    if not (last and k >= 2):
                        maxima(*ahead, t, True)
                    if t == 0 and b is NORMS and k == 3:
                        dve.wait_ge(flag_turned, 1)
                        dve.tensor_reduce(low_flag[:, :], tr_ps[0:1, 0:P], AX.X, ALU.max).then_inc(flag_done, 1)
                    if t == 1 and norming and k < 2:
                        batch_moments(b + 2, k, k == 0)
                    if t == 1 and not (first and k == 0):
                        if k == 1 and not first:
                            dve.wait_ge(x1_done, b)
                        divide(u - 1, (k - 1) % UNITS)
                if not (last and k >= 2):
                    split_maxima(u + 2, k, True)
                if norming:
                    dve.wait_ge(w_in, 16 * (b + 1))
                    if not (first and k == 0):
                        dve.wait_ge(w_seen, UNITS * b + k)
                    dve.tensor_tensor(bits[:, :], bits[:, :], w_stage[:, k * WQ:(k + 1) * WQ].bitcast(I32),
                                      ALU.bitwise_or).then_inc(w_seen, 1)
                if b is NORMS and k == 0:
                    dve.wait_ge(w_seen, WPIECES * UNITS)
                    dve.tensor_scalar(low_bits[:, :], bits[:, :], LOW_BITS, None, ALU.bitwise_and).then_inc(flag_step, 1)
                    dve.wait_ge(flag_step, 1)
                    dve.tensor_reduce(low_col[:, :], low_bits[:, :], AX.X, ALU.max).then_inc(flag_step, 1)

            for k in range(UNITS):
                step(0, k, True, False)
            with dve.Fori(1, NORMS) as b:
                for k in range(UNITS):
                    step(b, k, False, False)
            def chunk_moments(c, t):
                dve.wait_ge(c_in, 16 * (c + 1))
                if t == 0:
                    dve.wait_ge(x_normed, ST * B)
                tile_moments(c_ln, t, ST * B + CT * c + t, t)

            def rows_low(c, m, slot):
                dve.wait_ge(c_hi_done, 2 * c + m + 1)
                dve.tensor_tensor(xt_lo[:, 2 * m:2 * m + 2, :], gu_ps[slot][:, :, :],
                                  xt_hi[:, 2 * m:2 * m + 2, :].bitcast(F32), ALU.subtract).then_inc(c_lo_done, 1)

            def hidden(c, i):
                n = IT * c + i
                slot = i % 2
                hs = i % HS
                dve.wait_ge(th_done, n + 1)
                dve.scalar_tensor_tensor(silu2[slot][:, :], th[slot][:, :], 1.0, gu_ps[slot][:, 0, :],
                                         ALU.add, ALU.mult).then_inc(silu_done, 1)
                dve.wait_ge(silu_done, n + 1)
                if i >= HS:
                    dve.wait_ge(hid_lo_done, n - HS + 1)
                dve.scalar_tensor_tensor(hid[hs][:, :], silu2[slot][:, :], hid_scale[:, i:i + 1], gu_ps[slot][:, 1, :],
                                         ALU.mult, ALU.mult).then_inc(hid_done, 1)

            def output(c):
                dve.wait_ge(cr_in, 16 * (c + 1))
                for t in range(CT):
                    dve.wait_ge(acc_done, CT * c + t + 1)
                    dve.tensor_tensor(y_sb[:, t, :], acc_ps[t][:, :], down_gate[:, :], ALU.mult).then_inc(y_done, 1)

            def chunk(c, last):
                for i in range(IT):
                    hidden(c, i)
                    if not last and 3 <= i < 3 + CT:
                        chunk_moments(c + 1, i - 3)
                if not last:
                    rows_low(c + 1, 0, 1)
                    rows_low(c + 1, 1, 0)
                output(c)

            for b in (NORMS, LAST):
                for k in range(UNITS):
                    step(b, k, False, b == LAST)
                    if b == LAST and k < 2:
                        for t in range(2 * k, 2 * k + 2):
                            chunk_moments(0, t)
                    if b == LAST and k == 3:
                        rows_low(0, 0, 1)
            rows_low(0, 1, 0)
            divide(UNITS * B - 1, UNITS - 1)

            with dve.Fori(0, NCH - 1) as c:
                chunk(c, False)
            chunk(NCH - 1, True)

        @block.scalar
        def _(act):
            act.wait_ge(gates_in, 32)
            act.activation(tgates[:, :], gates[:, :], ACT.Tanh).then_inc(tanh_done, 1)

            def queries_high(b, c, reused):
                act.wait_ge(qt_copied, 2 * b + c + 1)
                if reused:
                    act.wait_ge(qt_stored[c], 64 * b)
                act.activation(qt_hi[c][:, :, :], qt[:, :, :], ACT.Copy).then_inc(qt_hi_done, 1)

            def copy_queries(b, c):
                act.wait_ge(qt_turned, 2 * b + c + 1)
                if not (isinstance(b, int) and b == 0 and c == 0):
                    act.wait_ge(qt_lo_done, 2 * b + c)
                act.activation(qt[:, :, :], tr_ps[:, :].rearrange("p (j s) -> p j s", j=2), ACT.Copy).then_inc(qt_copied, 1)

            def copy_maxima(u, k, reused):
                act.wait_ge(m_turned, u + 1)
                if reused:
                    act.wait_ge(m_in, 16 * (u - 1))
                act.activation(m_rows[k % 2][:, :], tr_ps[0:2 * UH * ST, 0:P], ACT.Copy).then_inc(m_copied, 1)

            def exponents(u, j, reused):
                tt, i = divmod(j, PAIRS)
                act.wait_ge(t_done, 2 * PAIRS * u + j + 1)
                if i == 0 and reused:
                    act.wait_ge(pv_done, TT * (u - 1) + tt + 1)
                act.activation(probs[:, tt, i, :], t_ps[j % 2][:, :], ACT.Exp, scale=RSCALE).then_inc(exp_done, 1)

            def copy_output(u):
                act.wait_ge(pv_done, TT * (u + 1))
                act.activation(o_sb[:, :], o_ps[:, :], ACT.Copy).then_inc(o_copied, 1)

            for b in range(2):
                for c in range(2):
                    copy_queries(b, c)
                    queries_high(b, c, b == 1)
            copy_maxima(0, 0, False)

            def step(b, k, first, last):
                u = UNITS * b + k
                turned_before = k == 3 and not last and b is not NORMS or k == 0 and not first and not last
                for j in range(2 * PAIRS):
                    if j == 0 and turned_before:
                        queries_high(*((b + 2, 0) if k else (b + 1, 1)), True)
                    exponents(u, j, not (first and k == 0))
                    if j == 1 and not (first and k == 0):
                        copy_output(u - 1)
                    if j == 2 and not (last and k == 3):
                        copy_maxima(u + 1, k + 1, not (first and k == 0))
                    if j == 7 and k >= 2 and not last and b is not NORMS:
                        copy_queries(b + 2, k - 2)

            for k in range(UNITS):
                step(0, k, True, False)
            with act.Fori(1, NORMS) as b:
                for k in range(UNITS):
                    step(b, k, False, False)
            def rows_high(c, m, slot):
                act.wait_ge(c_turned, 2 * c + m + 1)
                act.activation(xt_hi[:, 2 * m:2 * m + 2, :], gu_ps[slot][:, :, :], ACT.Copy).then_inc(c_hi_done, 1)

            def half_tanh(c, i):
                act.wait_ge(gu_done, IT * c + i + 1)
                act.activation(th[i % 2][:, :], gu_ps[i % 2][:, 0, :], ACT.Tanh,
                               scale=half_gs[:, i:i + 1]).then_inc(th_done, 1)

            def hidden_high(c, i):
                n = IT * c + i
                act.wait_ge(hid_done, n + 1)
                if i >= HS:
                    act.wait_ge(down_done, (IT - 1) * c + i - HS + 1)
                act.activation(hid_hi[i % HS][:, :], hid[i % HS][:, :], ACT.Copy).then_inc(hid_hi_done, 1)

            def chunk(c, last):
                for i in range(IT):
                    if i:
                        hidden_high(c, i - 1)
                    half_tanh(c, i)
                hidden_high(c, IT - 1)
                if not last:
                    rows_high(c + 1, 0, 1)
                    rows_high(c + 1, 1, 0)

            for b in (NORMS, LAST):
                for k in range(UNITS):
                    step(b, k, False, b == LAST)
                    if b == LAST and k == 2:
                        for h in range(2):
                            act.wait_ge(qt_stored[h], 64 * B)
                        rows_high(0, 0, 1)
            rows_high(0, 1, 0)
            copy_output(UNITS * B - 1)

            with act.Fori(0, NCH - 1) as c:
                chunk(c, False)
            chunk(NCH - 1, True)

        @block.tensor
        def _(pe):
            def turn_queries(b, c):
                pe.wait_ge(x_normed, ST * (b + 1))
                for j in range(2):
                    for st in range(ST):
                        at = j * S + st * P
                        mm = pe.transpose(tr_ps[:, at:at + P], x_norm[:, st, (2 * c + j) * P:(2 * c + j + 1) * P], ident[:, :])
                mm.then_inc(qt_turned, 1)

            def scores(b, k, j, reused):
                u = UNITS * b + k
                h, t = k // 2, j // 2
                if j == 0:
                    pe.wait_ge(q_in[k], 32 * (b + 1))
                    pe.wait_ge(k_max_done, 2 * b + h + 1)
                if j % 2 == 0 and reused:
                    pe.wait_ge(max_done, 4 * u + t - 1)
                for st in range(ST):
                    mm = pe.matmul(s_ps[t % 2][:, ST * (j % 2) + st, :], q_st[k][0:SROWS, j, st * P:(st + 1) * P],
                                   k_max[h][0:SROWS, kv_of(k, j // UG), :], start=True, stop=True)
                if j % 2:
                    mm.then_inc(s_done, 1)

            def turn_maxima(u, k):
                pe.wait_ge(m_lo_done, u + 1)
                pe.transpose(tr_ps[0:2 * UH * ST, 0:P], m_parts[k % 2][:, :, :].rearrange("p a n -> p (a n)").bitcast(F32),
                             ident[:, :]).then_inc(m_turned, 1)

            def shifted(b, k, j, reused):
                u = UNITS * b + k
                h = k // 2
                tt, i = divmod(j, PAIRS)
                if j == 0:
                    pe.wait_ge(m_in, 16 * (u + 1))
                    pe.wait_ge(k_exp_done, 2 * b + h + 1)
                if reused:
                    pe.wait_ge(exp_done, 2 * PAIRS * u + j - 1)
                pe.matmul(t_ps[j % 2][:, :], k_exp[h][0:DROWS, kv_of(k, i), tt * P:(tt + 1) * P],
                          q_st[k][0:DROWS, UG * i:UG * i + UG, :].rearrange("p g s -> p (g s)"),
                          start=True, stop=True).then_inc(t_done, 1)

            def weigh(b, k, tt, reused):
                u = UNITS * b + k
                h = k // 2
                pe.wait_ge(exp_done, 2 * PAIRS * u + PAIRS * (tt + 1))
                if tt == 0:
                    pe.wait_ge(v_done, TT * (2 * b + h + 1))
                    if reused:
                        pe.wait_ge(o_copied, u)
                for i in range(PAIRS):
                    mm = pe.matmul(o_ps[i * VW:(i + 1) * VW, :], v_aug[h][:, tt, kv_of(k, i), :], probs[:, tt, i, :],
                                   start=(tt == 0), stop=(tt == TT - 1))
                mm.then_inc(pv_done, 1)

            def turn_output(u):
                pe.wait_ge(o_copied, u + 1)
                for j in range(UG * ST):
                    mm = pe.transpose(tr_ps[:, j * P:(j + 1) * P], o_sb[:, j * P:(j + 1) * P], ident[:, :])
                mm.then_inc(o_turned, 1)

            def turn_rows(c, m, slot):
                pe.wait_ge(c_normed, CT * (c + 1))
                for kk in range(2):
                    for t in range(CT):
                        k = 2 * m + kk
                        mm = pe.transpose(gu_ps[slot][:, kk, t * P:(t + 1) * P], c_norm[:, t, k * P:(k + 1) * P],
                                          ident[:, :])
                mm.then_inc(c_turned, 1)

            pe.wait_ge(ident_done, 1)
            for b in range(2):
                for c in range(2):
                    if b or c:
                        pe.wait_ge(qt_copied, 2 * b + c)
                    turn_queries(b, c)
            for k in range(2):
                for j in range(UH):
                    scores(0, k, j, k > 0 or j >= 4)
                if k == 0:
                    pe.wait_ge(qt_copied, 4)
                    turn_maxima(0, 0)

            def step(b, k, first, last):
                u = UNITS * b + k
                norming = not last and b is not NORMS
                ahead = (b, k + 2) if k < 2 else (b + 1, k - 2)
                started = not (first and k == 0)
                for j in range(UH):
                    shifted(b, k, j, started or j >= 2)
                    if j == 1 and started:
                        weigh(*((b, k - 1) if k else (b - 1, UNITS - 1)), 1, True)
                    if j == 4 and started:
                        if last and k == 3:
                            pe.wait_ge(o_normed, u - 1)
                        else:
                            pe.wait_ge(m_copied, u + 2)
                        turn_output(u - 1)
                    if j == 5:
                        weigh(b, k, 0, started)
                    if not (last and k >= 2):
                        scores(*ahead, j, True)
                    if j == 2 and not (last and k == 3):
                        if norming and k == 3:
                            pe.wait_ge(qt_copied, 2 * (b + 2) + 1)
                        elif k == 0 and not first and not last:
                            pe.wait_ge(qt_copied, 2 * (b + 1) + 2)
                        elif b is NORMS and k == 3:
                            pe.wait_ge(flag_done, 1)
                        elif first and k < 2:
                            pe.wait_ge(m_copied, u + 1)
                        else:
                            pe.wait_ge(o_normed, u - 1)
                        turn_maxima(u + 1, k + 1)
                    if j == 7 and norming and k >= 2:
                        pe.wait_ge(o_normed, u)
                        turn_queries(b + 2, k - 2)
                    if j == 7 and b is NORMS and k == 2:
                        pe.wait_ge(o_normed, u)
                        pe.wait_ge(flag_step, 2)
                        pe.transpose(tr_ps[0:1, 0:P], low_col[:, :], ident[:, :]).then_inc(flag_turned, 1)

            for k in range(UNITS):
                step(0, k, True, False)
            with pe.Fori(1, NORMS) as b:
                for k in range(UNITS):
                    step(b, k, False, False)
            for b in (NORMS, LAST):
                for k in range(UNITS):
                    step(b, k, False, b == LAST)
                    if b == LAST and k == 1:
                        pe.wait_ge(max_done, 4 * UNITS * B)
                    if b == LAST and k >= 2:
                        turn_rows(0, k - 2, 3 - k)
            weigh(LAST, UNITS - 1, 1, True)
            pe.wait_ge(o_normed, UNITS * B - 1)
            turn_output(UNITS * B - 1)

            TURNS = IT + 2

            def free_slots(c, used):
                if used <= 2:
                    pe.wait_ge(c_lo_done, 2 * c + used)
                else:
                    pe.wait_ge(hid_done, IT * c + used - 2)

            def feed_forward(kind):
                def as_kind(ap):
                    return ap if kind == F32R else ap.bitcast(kind)

                def gate_up(c, i):
                    slot = i % 2
                    free_slots(c, 2 if i == 0 else i + 1)
                    for half, w in ((0, gate_w), (1, up_w)):
                        for k in range(KT):
                            for part in (xt_hi, xt_lo):
                                mm = pe.matmul(gu_ps[slot][:, half, :], as_kind(w[:, k, i * P:(i + 1) * P]),
                                               as_kind(part[:, k, :]), start=(k == 0 and part is xt_hi),
                                               stop=(k == KT - 1 and part is xt_lo))
                    mm.then_inc(gu_done, 1)

                def down(c, i):
                    pe.wait_ge(hid_lo_done, IT * c + i + 1)
                    for t in range(CT):
                        for part in (hid_hi, hid_lo):
                            mm = pe.matmul(acc_ps[t][:, :], as_kind(part[i % HS][:, t * P:(t + 1) * P]),
                                           as_kind(down_w[:, i, :]), start=(i == 0 and part is hid_hi),
                                           stop=(i == IT - 1 and part is hid_lo))
                        if i == IT - 1:
                            mm.then_inc(acc_done, 1)
                    if i < IT - 1:
                        mm.then_inc(down_done, 1)

                def chunk(c, last):
                    for i in range(IT - 1):
                        gate_up(c, i)
                        if i >= LAG:
                            down(c, i - LAG)
                    gate_up(c, IT - 1)
                    down(c, IT - 3)
                    if not last:
                        free_slots(c, IT + 1)
                        turn_rows(c + 1, 0, 1)
                        free_slots(c, IT + 2)
                        turn_rows(c + 1, 1, 0)
                    down(c, IT - 2)
                    down(c, IT - 1)

                with pe.Fori(0, NCH - 1) as c:
                    chunk(c, False)
                chunk(NCH - 1, True)

            pe.wait_ge(o_normed, UNITS * B)
            pe.wait_ge(w_set, 16 * WPIECES)
            pe.wait_ge(flag_done, 1)
            inexact = pe.value_load(low_flag[0:1, 0:1])
            with pe.If(inexact == 0):
                feed_forward(F32R)
            with pe.Else():
                feed_forward(F32)


_INS = ["x", "ctx_n", "ctx_t", "g_xattn", "g_ffn", "weights", "gate_s", "up_s", "down_s"]


def kernel(x, ctx_512, g_xattn, g_ffn, L0_ffn_gate_w, L0_ffn_up_w, L0_ffn_down_w, L0_ffn_gate_s, L0_ffn_up_s,
           L0_ffn_down_s):
    import concourse.bacc as bacc
    from concourse.bass_utils import run_bass_kernel_spmd

    def rows_on_partitions(w):
        n = w.shape[0] // P
        return w.reshape(n, P, w.shape[1]).transpose(1, 0, 2).reshape(P, -1)

    ctx = np.asarray(ctx_512)
    arrays = {
        "x": np.asarray(x), "ctx_n": ctx, "ctx_t": ctx.reshape(B * T, KV * D).T,
        "g_xattn": np.asarray(g_xattn), "g_ffn": np.asarray(g_ffn),
        "weights": np.concatenate([rows_on_partitions(np.asarray(w).T)
                                   for w in (L0_ffn_gate_w, L0_ffn_up_w, L0_ffn_down_w)], axis=1),
        "gate_s": np.asarray(L0_ffn_gate_s).reshape(IT, P).T, "up_s": np.asarray(L0_ffn_up_s).reshape(IT, P).T,
        "down_s": np.asarray(L0_ffn_down_s),
    }
    nc = bacc.Bacc("TRN2", target_bir_lowering=False, num_devices=1)
    args = []
    for name in _INS:
        arrays[name] = np.ascontiguousarray(arrays[name])
        args.append(nc.dram_tensor(name, arrays[name].shape, F32, kind="ExternalInput").ap())
    out = nc.dram_tensor("out", [B, S, E], F32, kind="ExternalOutput").ap()
    build(nc, *args, out)
    r = run_bass_kernel_spmd(nc, [arrays], core_ids=[0])
    return r.results[0]["out"]
```

```python
import numpy as np
import concourse.bass as bass
from concourse import mybir
from contextlib import ExitStack

F32 = mybir.dt.float32
F32R = mybir.dt.float32r
I32 = mybir.dt.int32
ALU = mybir.AluOpType
ACT = mybir.ActivationFunctionType
AX = mybir.AxisListType

P = 128
B, S, E = 8, 256, 512
T = 256
H, KV, D = 32, 8, 16
G = H // KV
ST = S // P
TT = T // P
UNITS = 4
PAIRS, UG = 4, 2
UH = PAIRS * UG
UKV = KV // 2
NPART = 4
ZROW = NPART * D
HIROW, LOROW = ZROW + 1, ZROW + 2
SROWS, DROWS = ZROW + 1, ZROW + 3
VW = 32
F = 1408
IT = F // P
KT = E // P
CH = 512
CT = CH // P
NCH = B * S // CH
HS = 3
LAG = 2
WCOLS = 3 * KT * F
WPIECES = 6
WP = WCOLS // WPIECES
WCUT = [0, 1024, 1920, WP]
EPS = 1e-5
LOW_BITS = 0xFFF
WARMUP, BUSY = 24, 4
RSCALE = 1.0 / float(D) ** 0.5


def kv_of(k, pair):
    return (k % 2) * 2 + pair // 2


def build(nc, x, ctx_n, ctx_t, g_xattn, g_ffn, weights, gate_s, up_s, down_s, out):
    q_parts = nc.dram_tensor("q_parts", [B, 2, UH, D, 2, 2, S], F32).ap()
    x1_dram = nc.dram_tensor("x1_scratch", [B * S, E], F32).ap()

    with ExitStack() as top:
        def sem(name):
            return top.enter_context(nc.semaphore(name))

        def sb(stack, name, shape, dt=F32):
            return stack.enter_context(nc.sbuf_tensor(name, shape, dt))

        def ps(stack, name, shape, dt=F32):
            return stack.enter_context(nc.psum_tensor(name, shape, dt))

        w_sb = sb(top, "w_sb", [P, WCOLS], F32R)
        ident = sb(top, "ident", [P, P])
        ident_zero = sb(top, "ident_zero", [P, P])
        gates = sb(top, "gates", [P, 2])
        tgates = sb(top, "tgates", [P, 2])
        gs_col = sb(top, "gs_col", [P, IT])
        us_col = sb(top, "us_col", [P, IT])
        half_gs = sb(top, "half_gs", [P, IT])
        hid_scale = sb(top, "hid_scale", [P, IT])
        down_row = sb(top, "down_row", [P, E])
        down_gate = sb(top, "down_gate", [P, E])
        bits = sb(top, "bits", [P, WCUT[1]], I32)
        low_bits = sb(top, "low_bits", [P, WCUT[1]], I32)
        low_col = sb(top, "low_col", [P, 1])
        low_flag = sb(top, "low_flag", [1, 1], I32)
        minus_half = sb(top, "minus_half", [P, CT])
        stats = sb(top, "stats", [P, CT, 6])
        moments = sb(top, "moments", [P, CT, 2])
        var_eps = sb(top, "var_eps", [P, CT])
        rstd = sb(top, "rstd", [P, CT])
        mean_rstd = sb(top, "mean_rstd", [P, CT])
        shift = sb(top, "shift", [P, CT])

        attn = sb(top, "attn", [P, ST, E])
        x_res = sb(top, "x_res", [P, ST, E])

        att = ExitStack()
        w_stage = sb(att, "w_stage", [P, WP])
        x_ln = sb(att, "x_ln", [P, ST, E])
        x_norm = sb(att, "x_norm", [P, ST, E])
        k_raw = sb(att, "k_raw", [ZROW, KV, T])
        qt = sb(att, "qt", [P, 2, S])
        qt_parts = [sb(att, f"qt_parts{h}", [P, 2, 2, S], F32R) for h in range(2)]
        q_st = [sb(att, f"q_st{k}", [DROWS, UH, S], F32R) for k in range(UNITS)]
        k_max = [sb(att, f"k_max{h}", [DROWS, UKV, T], F32R) for h in range(2)]
        k_exp = [sb(att, f"k_exp{h}", [DROWS, UKV, T], F32R) for h in range(2)]
        v_raw = sb(att, "v_raw", [P, TT, KV * D])
        v_aug = [sb(att, f"v_aug{h}", [P, TT, UKV, VW]) for h in range(2)]
        probs = sb(att, "probs", [P, TT, PAIRS, UG * S])
        o_sb = sb(att, "o_sb", [P, UG * S])
        rden = sb(att, "rden", [P, UG * ST, PAIRS])
        negmax = [sb(att, f"negmax{h}", [P, UH * ST]) for h in range(2)]
        m_parts = [sb(att, f"m_parts{h}", [P, 2, UH * ST], F32R) for h in range(2)]
        m_rows = [sb(att, f"m_rows{h}", [2 * UH * ST, P]) for h in range(2)]
        s_ps = [ps(att, f"s_ps{h}", [P, 2 * ST, T]) for h in range(2)]
        t_ps = [ps(att, f"t_ps{h}", [P, UG * S]) for h in range(2)]
        o_ps = ps(att, "o_ps", [P, UG * S])
        tr_ps = ps(att, "tr_ps", [P, 2 * S])
        att.close()

        ffn = ExitStack()
        c_ln = sb(ffn, "c_ln", [P, CT, E])
        c_norm = sb(ffn, "c_norm", [P, CT, E])
        xt_hi = sb(ffn, "xt_hi", [P, KT, CH], F32R)
        xt_lo = sb(ffn, "xt_lo", [P, KT, CH], F32R)
        c_res = sb(ffn, "c_res", [P, CT, E])
        th = [sb(ffn, f"th{h}", [P, CH]) for h in range(2)]
        silu2 = [sb(ffn, f"silu2{h}", [P, CH]) for h in range(2)]
        hid = [sb(ffn, f"hid{h}", [P, CH]) for h in range(HS)]
        hid_hi = [sb(ffn, f"hid_hi{h}", [P, CH], F32R) for h in range(HS)]
        hid_lo = [sb(ffn, f"hid_lo{h}", [P, CH], F32R) for h in range(HS)]
        y_sb = sb(ffn, "y_sb", [P, CT, E])
        gu_ps = [ps(ffn, f"gu_ps{h}", [P, 2, CH]) for h in range(2)]
        acc_ps = [ps(ffn, f"acc_ps{t}", [P, E]) for t in range(CT)]
        ffn.close()

        gates_in = sem("gates_in")
        scales_in = sem("scales_in")
        filled = sem("filled")
        padded = sem("padded")
        ident_done = sem("ident_done")
        tanh_done = sem("tanh_done")
        scales_done = sem("scales_done")
        x_in = sem("x_in")
        stat_done = sem("stat_done")
        moments_done = sem("moments_done")
        norm_chain = sem("norm_chain")
        x_normed = sem("x_normed")
        qt_turned = sem("qt_turned")
        qt_copied = sem("qt_copied")
        qt_hi_done = sem("qt_hi_done")
        qt_lo_done = sem("qt_lo_done")
        qt_stored = [sem(f"qt_stored{h}") for h in range(2)]
        q_in = [sem(f"q_in{k}") for k in range(UNITS)]
        k_in = sem("k_in")
        k_hi_done = sem("k_hi_done")
        k_max_done = sem("k_max_done")
        k_exp_done = sem("k_exp_done")
        v_in = sem("v_in")
        v_done = sem("v_done")
        s_done = sem("s_done")
        max_done = sem("max_done")
        m_hi_done = sem("m_hi_done")
        m_lo_done = sem("m_lo_done")
        m_turned = sem("m_turned")
        m_copied = sem("m_copied")
        m_in = sem("m_in")
        t_done = sem("t_done")
        exp_done = sem("exp_done")
        pv_done = sem("pv_done")
        o_copied = sem("o_copied")
        o_turned = sem("o_turned")
        rden_done = sem("rden_done")
        o_normed = sem("o_normed")
        r_in = sem("r_in")
        gated_done = sem("gated_done")
        x1_done = sem("x1_done")
        x1_stored = sem("x1_stored")
        w_in = sem("w_in")
        w_seen = sem("w_seen")
        w_set = sem("w_set")
        flag_step = sem("flag_step")
        flag_turned = sem("flag_turned")
        flag_done = sem("flag_done")
        c_in = sem("c_in")
        c_normed = sem("c_normed")
        c_turned = sem("c_turned")
        c_hi_done = sem("c_hi_done")
        c_lo_done = sem("c_lo_done")
        gu_done = sem("gu_done")
        th_done = sem("th_done")
        silu_done = sem("silu_done")
        hid_done = sem("hid_done")
        hid_hi_done = sem("hid_hi_done")
        hid_lo_done = sem("hid_lo_done")
        down_done = sem("down_done")
        acc_done = sem("acc_done")
        y_done = sem("y_done")
        cr_in = sem("cr_in")
        out_ready = sem("out_ready")
        last_ready = sem("last_ready")
        out_stored = sem("out_stored")

        sp_passed, pool_passed, dve_passed = sem("sp_passed"), sem("pool_passed"), sem("dve_passed")

        block = top.enter_context(nc.Block())

        kt_view = ctx_t.rearrange("(v d) (b t) -> b d v t", d=D, b=B)
        v_view = ctx_n.rearrange("b (tt p) e -> b p tt e", p=P)
        x_view = x.rearrange("b (st p) e -> b p st e", p=P)
        x1w_view = x1_dram.rearrange("(b st p) e -> b p st e", p=P, st=ST)
        x1c_view = x1_dram.rearrange("(c ct p) e -> c p ct e", p=P, ct=CT)
        out_view = out.rearrange("b s e -> (b s) e").rearrange("(c ct p) e -> c p ct e", p=P, ct=CT)
        gate_w = w_sb[:, 0:KT * F].rearrange("p (k i) -> p k i", k=KT)
        up_w = w_sb[:, KT * F:2 * KT * F].rearrange("p (k i) -> p k i", k=KT)
        down_w = w_sb[:, 2 * KT * F:WCOLS].rearrange("p (i h) -> p i h", i=IT)
        attn_units = attn[:, :, :].rearrange("p st (k i g d) -> p k g st i d", k=UNITS, i=PAIRS, g=UG)

        def waited(engine, passed):
            engine.sem_inc(passed)

        LAST = B - 1
        NORMS = B - 2

        @block.sync
        def _(sp):
            def load_x(b):
                sp.dma_start(x_ln[:, :, :], x_view[b]).then_inc(x_in, 16)

            def load_k(b):
                for r in range(2):
                    for part in range(2):
                        at = r * 2 * D + part
                        sp.dma_start(k_raw[at:at + 2 * D - 1:2, :, :], kt_view[b]).then_inc(k_in, 16)

            def load_v(b):
                sp.dma_start(v_raw[:, :, :], v_view[b]).then_inc(v_in, 16)

            def store_q(b, c):
                sp.wait_ge(qt_lo_done, 2 * b + c + 1)
                sp.dma_start(q_parts[b, c].rearrange("h d part j s -> (h d) part j s"),
                             qt_parts[c][:, :, :, :].bitcast(F32)).then_inc(qt_stored[c], 16)

            def load_q(b, k, reused):
                sp.wait_ge(qt_stored[k // 2], 16 * (b + 1))
                if reused:
                    waited(sp, sp_passed)
                    sp.wait_ge(t_done, 2 * PAIRS * (UNITS * (b - 1) + k + 1))
                waited(sp, sp_passed)
                src = q_parts[b, k // 2, :, :, :, k % 2, :].rearrange("h d part s -> (d part) h s")
                for r in range(2):
                    sp.dma_start(q_st[k][r * 2 * D:(r + 1) * 2 * D, :, :].bitcast(F32), src).then_inc(q_in[k], 16)

            def place_maxima(b, k):
                sp.wait_ge(m_copied, UNITS * b + k + 1)
                sp.dma_start(q_st[k][HIROW:LOROW + 1, :, :].bitcast(F32), m_rows[k % 2][:, :]).then_inc(m_in, 16)

            load_x(0)
            load_k(0)
            sp.wait_ge(x_normed, ST)
            load_x(1)
            store_q(0, 0)
            for k in range(2):
                load_q(0, k, False)
            store_q(0, 1)
            load_q(0, 2, False)
            load_v(0)
            sp.dma_start(gates[:, 0:1], g_xattn.partition_broadcast(P)).then_inc(gates_in, 16)
            sp.dma_start(gates[:, 1:2], g_ffn.partition_broadcast(P)).then_inc(gates_in, 16)
            load_q(0, 3, False)
            sp.wait_ge(x_normed, 2 * ST)
            load_x(2)
            store_q(1, 0)
            place_maxima(0, 0)
            sp.wait_ge(k_max_done, 2)
            load_k(1)
            sp.dma_start(gs_col[:, :], gate_s).then_inc(scales_in, 16)
            sp.dma_start(us_col[:, :], up_s).then_inc(scales_in, 16)
            sp.dma_start(down_row[:, :], down_s.partition_broadcast(P)).then_inc(scales_in, 16)

            def step(b, k, first, last):
                norming = not last and b is not NORMS
                if k == 0:
                    if not first:
                        load_q(b, 3, True)
                elif not last:
                    load_q(b + 1, k - 1, True)
                if k < 3:
                    place_maxima(b, k + 1)
                elif not last:
                    place_maxima(b + 1, 0)
                if k == 2 and not last:
                    sp.wait_ge(v_done, 2 * TT * (b + 1))
                    load_v(b + 1)
                if k == 2 and not first:
                    sp.wait_ge(x1_done, b)
                    sp.dma_start(x1w_view[b - 1], x_res[:, :, :]).then_inc(x1_stored, 16)
                if k == 0 and not first:
                    sp.dma_start(x_res[:, :, :], x_view[b - 1]).then_inc(r_in, 16)
                if k == 3 and not first:
                    sp.wait_ge(x1_stored, 16 * b)
                    waited(sp, sp_passed)
                if k == 3 and last:
                    sp.dma_start(x_res[:, :, :], x_view[b]).then_inc(r_in, 16)
                if k == 0 and first:
                    store_q(1, 1)
                if k == 3 and norming:
                    sp.wait_ge(k_max_done, 2 * (b + 2))
                    load_k(b + 2)
                if b is NORMS and k == 1:
                    sp.wait_ge(w_seen, 3 * WPIECES)
                    sp.wait_ge(w_set, 16 * 3 * WPIECES)
                    sp.wait_ge(x_normed, ST * B)
                    sp.dma_start(c_ln[:, :, :], x1c_view[0]).then_inc(c_in, 16)
                if norming and k:
                    n = WCUT[k] - WCUT[k - 1]
                    sp.wait_ge(w_in, 16 * (3 * b + k))
                    if not (first and k == 1):
                        waited(sp, sp_passed)
                        sp.wait_ge(w_set, 16 * (3 * b + k - 1))
                    waited(sp, sp_passed)
                    sp.dma_start(w_sb[:, bass.ds(b * WP + WCUT[k - 1], n)].bitcast(F32),
                                 w_stage[:, WCUT[k - 1]:WCUT[k]]).then_inc(w_set, 16)
                if norming and k < 3:
                    if not first:
                        sp.wait_ge(w_seen, 3 * (b - 1) + k + 1)
                        if k == 0:
                            waited(sp, sp_passed)
                            sp.wait_ge(w_set, 16 * 3 * b)
                    waited(sp, sp_passed)
                    n = WCUT[k + 1] - WCUT[k]
                    sp.dma_start(w_stage[:, WCUT[k]:WCUT[k + 1]],
                                 weights[:, bass.ds(b * WP + WCUT[k], n)]).then_inc(w_in, 16)
                if k == 3 and norming:
                    store_q(b + 2, 0)
                if k == 0 and not first and not last:
                    store_q(b + 1, 1)

            def next_x(b, k):
                if k == 1:
                    sp.wait_ge(x_normed, ST * (b + 3))
                    load_x(b + 3)

            for k in range(UNITS):
                step(0, k, True, False)
                next_x(0, k)
            with sp.Fori(1, NORMS - 1) as b:
                for k in range(UNITS):
                    step(b, k, False, False)
                    next_x(b, k)
            for k in range(UNITS):
                step(NORMS - 1, k, False, False)
            for b in (NORMS, LAST):
                for k in range(UNITS):
                    step(b, k, False, b == LAST)
            sp.wait_ge(x1_done, B)
            sp.dma_start(x1w_view[LAST], x_res[:, :, :]).then_inc(x1_stored, 16)

            sp.wait_ge(x1_stored, 16 * B)

            def load_chunk(c):
                sp.dma_start(c_ln[:, :, :], x1c_view[c]).then_inc(c_in, 16)

            def load_residual(c):
                sp.dma_start(c_res[:, :, :], x1c_view[c]).then_inc(cr_in, 16)

            def store_out(c, last):
                for t in range(CT):
                    if last and t >= CT // 2:
                        sp.wait_ge(last_ready, t - CT // 2 + 1)
                    else:
                        sp.wait_ge(out_ready, CT * c + t + 1)
                    sp.dma_start(out_view[c, :, t, :], y_sb[:, t, :]).then_inc(out_stored, 16)

            load_residual(0)
            with sp.Fori(0, NCH - 1) as c:
                sp.wait_ge(c_normed, CT * (c + 1))
                load_chunk(c + 1)
                store_out(c, False)
                sp.wait_ge(out_stored, 16 * CT * (c + 1))
                load_residual(c + 1)
            store_out(NCH - 1, True)
            sp.wait_ge(out_stored, 16 * CT * NCH)

        @block.gpsimd
        def _(pool):
            pool.memset(ident_zero[:, :], 0.0).then_inc(filled, 1)
            pool.wait_ge(filled, 1)
            pool.affine_select(out=ident[:, :], in_=ident_zero[:, :], compare_op=ALU.not_equal, fill=1.0, base=0,
                               pattern=[[-1, P]], channel_multiplier=1).then_inc(ident_done, 1)
            pool.memset(minus_half[:, :], -0.5).then_inc(filled, 1)
            for n, keys in enumerate((k_max[0], k_exp[0], k_max[1], k_exp[1])):
                pool.wait_ge(filled, n + 2)
                pool.memset(keys[ZROW:DROWS, :, :].bitcast(F32), 1.0).then_inc(filled, 1)

            def norm_tiles(rows, n, src, dst, tiles, done):
                pool.wait_ge(moments_done, tiles)
                waited(pool, pool_passed)
                pool.tensor_scalar(var_eps[:, 0:n], moments[:, 0:n, 1], 1.0, EPS, ALU.mult, ALU.add).then_inc(norm_chain, 1)
                pool.wait_ge(norm_chain, 4 * rows + 1)
                pool.tensor_tensor(rstd[:, 0:n], var_eps[:, 0:n], minus_half[:, 0:n], ALU.pow).then_inc(norm_chain, 1)
                pool.wait_ge(norm_chain, 4 * rows + 2)
                pool.tensor_tensor(mean_rstd[:, 0:n], moments[:, 0:n, 0], rstd[:, 0:n], ALU.mult).then_inc(norm_chain, 1)
                pool.wait_ge(norm_chain, 4 * rows + 3)
                waited(pool, pool_passed)
                pool.tensor_scalar(shift[:, 0:n], mean_rstd[:, 0:n], -1.0, 0.0, ALU.mult, ALU.add).then_inc(norm_chain, 1)
                pool.wait_ge(norm_chain, 4 * rows + 4)
                waited(pool, pool_passed)
                for t in range(n):
                    pool.tensor_scalar(dst[:, t, :], src[:, t, :], rstd[:, t:t + 1], shift[:, t:t + 1],
                                       ALU.mult, ALU.add).then_inc(done, 1)

            def norm_batch(b, reused):
                if reused:
                    pool.wait_ge(qt_turned, 2 * b)
                norm_tiles(b, ST, x_ln, x_norm, ST * (b + 1), x_normed)

            def queries_low(b, c, reused):
                pool.wait_ge(qt_hi_done, 2 * b + c + 1)
                if reused:
                    pool.wait_ge(qt_stored[c], 16 * b)
                pool.tensor_tensor(qt_parts[c][:, 1, :, :], qt[:, :, :], qt_parts[c][:, 0, :, :].bitcast(F32),
                                   ALU.subtract).then_inc(qt_lo_done, 1)

            def keys_high(b, h, reused):
                pool.wait_ge(k_in, 16 * NPART * (b + 1))
                if reused:
                    pool.wait_ge(s_done, PAIRS * (UNITS * (b - 1) + 2 * h + 2))
                    pool.wait_ge(k_exp_done, 2 * (b - 1) + h + 1)
                waited(pool, pool_passed)
                pool.tensor_scalar(k_max[h][0:ZROW, :, :], k_raw[:, h * UKV:(h + 1) * UKV, :], 1.0, 0.0,
                                   ALU.mult, ALU.add).then_inc(k_hi_done, 1)

            def keys_low(b, h):
                n = 2 * b + h
                half = slice(ZROW // 2, ZROW)
                pool.wait_ge(k_hi_done, n + 1)
                pool.tensor_tensor(k_max[h][half, :, :], k_raw[half, h * UKV:(h + 1) * UKV, :],
                                   k_max[h][half, :, :].bitcast(F32), ALU.subtract).then_inc(k_max_done, 1)
                pool.wait_ge(k_max_done, n + 1)

            def keys_for_max(b, h, reused):
                keys_high(b, h, reused)
                keys_low(b, h)

            def keys_for_exp(b, h, reused):
                pool.wait_ge(k_max_done, 2 * b + h + 1)
                if reused:
                    pool.wait_ge(t_done, 2 * PAIRS * (UNITS * (b - 1) + 2 * h + 2))
                waited(pool, pool_passed)
                pool.tensor_scalar(k_exp[h][0:ZROW, :, :], k_max[h][0:ZROW, :, :].bitcast(F32), 1.0, 0.0,
                                   ALU.mult, ALU.add).then_inc(k_exp_done, 1)

            def values(b, h, reused):
                pool.wait_ge(v_in, 16 * (b + 1))
                if reused:
                    pool.wait_ge(pv_done, TT * (UNITS * (b - 1) + 2 * h + 2))
                waited(pool, pool_passed)
                for tt in range(TT):
                    src = v_raw[:, tt, h * UKV * D:(h + 1) * UKV * D].rearrange("p (v d) -> p v d", d=D)
                    pool.tensor_scalar(v_aug[h][:, tt, :, 0:D], src, 1.0, 0.0, ALU.mult, ALU.add).then_inc(v_done, 1)

            def residual(b):
                pool.wait_ge(o_normed, UNITS * (b + 1))
                waited(pool, pool_passed)
                pool.tensor_scalar(attn[:, :, :], attn[:, :, :], tgates[:, 0:1], 0.0,
                                   ALU.mult, ALU.add).then_inc(gated_done, 1)
                pool.wait_ge(gated_done, b + 1)
                pool.wait_ge(r_in, 16 * (b + 1))
                pool.tensor_tensor(x_res[:, :, :], x_res[:, :, :], attn[:, :, :], ALU.add).then_inc(x1_done, 1)

            pool.wait_ge(filled, 6)
            norm_batch(0, False)
            keys_high(0, 0, False)
            queries_low(0, 0, False)
            pool.wait_ge(qt_lo_done, 1)
            keys_low(0, 0)
            queries_low(0, 1, False)
            norm_batch(1, True)
            keys_for_exp(0, 0, False)
            queries_low(1, 0, True)
            keys_for_max(0, 1, False)
            keys_for_exp(0, 1, False)
            for h in range(2):
                values(0, h, False)
            queries_low(1, 1, True)
            pool.wait_ge(tanh_done, 1)

            def step(b, k, first, last):
                norming = not last and b is not NORMS
                if k == 0:
                    if not first:
                        keys_for_exp(b, 1, True)
                    if not last:
                        keys_for_max(b + 1, 0, True)
                    if norming:
                        norm_batch(b + 2, True)
                if k == 1 and not first:
                    residual(b - 1)
                    values(b, 1, True)
                if k == 2 and not last:
                    keys_for_exp(b + 1, 0, True)
                    keys_for_max(b + 1, 1, True)
                if k == 3 and not last:
                    values(b + 1, 0, True)
                if k >= 2 and norming:
                    queries_low(b + 2, k - 2, True)

            for k in range(UNITS):
                step(0, k, True, False)
            with pool.Fori(1, NORMS) as b:
                for k in range(UNITS):
                    step(b, k, False, False)

            def norm_chunk(c, reused):
                pool.wait_ge(c_in, 16 * (c + 1))
                if reused:
                    pool.wait_ge(c_turned, 2 * c)
                else:
                    pool.wait_ge(qt_turned, 2 * B)
                norm_tiles(B + c, CT, c_ln, c_norm, ST * B + CT * (c + 1), c_normed)

            def hidden_low(n, slot):
                pool.wait_ge(hid_hi_done, n + 1)
                pool.tensor_tensor(hid_lo[slot][:, :], hid[slot][:, :], hid_hi[slot][:, :].bitcast(F32),
                                   ALU.subtract).then_inc(hid_lo_done, 1)

            def add_residual(c, t):
                pool.wait_ge(y_done, CT * c + t + 1)
                pool.wait_ge(cr_in, 16 * (c + 1))
                pool.tensor_tensor(y_sb[:, t, :], y_sb[:, t, :], c_res[:, t, :], ALU.add).then_inc(out_ready, 1)

            def chunk(c, last):
                for i in range(2, IT):
                    hidden_low(IT * c + i, i % HS)
                    if i == 7 and not last:
                        norm_chunk(c + 1, True)
                if last:
                    for t in range(CT // 2):
                        add_residual(c, t)
                else:
                    add_residual(c, 0)
                    add_residual(c, 1)
                    hidden_low(IT * (c + 1), 0)
                    add_residual(c, 2)
                    hidden_low(IT * (c + 1) + 1, 1)
                    add_residual(c, 3)

            for b in (NORMS, LAST):
                for k in range(UNITS):
                    step(b, k, False, b == LAST)
                    if b == LAST and k == 0:
                        norm_chunk(0, False)
            residual(LAST)

            hidden_low(0, 0)
            hidden_low(1, 1)
            with pool.Fori(0, NCH - 1) as c:
                chunk(c, False)
            chunk(NCH - 1, True)

        @block.vector
        def _(dve):
            def tile_moments(src, t, n, col):
                dve.bn_stats(stats[:, t, :], src[:, t, :]).then_inc(stat_done, 1)
                dve.wait_ge(stat_done, n + 1)
                waited(dve, dve_passed)
                dve.bn_aggr(moments[:, t, :], stats[:, t, :]).then_inc(moments_done, 1)

            def batch_moments(b, t, reused):
                dve.wait_ge(x_in, 16 * (b + 1))
                if reused:
                    dve.wait_ge(x_normed, ST * b)
                tile_moments(x_ln, t, ST * b + t, t)

            def maxima(b, k, t, reused):
                u = UNITS * b + k
                dve.wait_ge(s_done, PAIRS * u + t + 1)
                if t == 0 and reused:
                    dve.wait_ge(m_lo_done, u - 1)
                dve.tensor_reduce(negmax[k % 2][:, 4 * t:4 * t + 4], s_ps[t % 2][:, :, :], AX.X, ALU.max,
                                  negate=True).then_inc(max_done, 1)

            def round_maxima(u, k, reused):
                dve.wait_ge(max_done, 4 * (u + 1))
                if reused:
                    dve.wait_ge(m_turned, u - 1)
                waited(dve, dve_passed)
                dve.tensor_copy(m_parts[k % 2][:, 0, :], negmax[k % 2][:, :]).then_inc(m_hi_done, 1)

            def maxima_low(u, k):
                dve.wait_ge(m_hi_done, u + 1)
                dve.tensor_tensor(m_parts[k % 2][:, 1, :], negmax[k % 2][:, :], m_parts[k % 2][:, 0, :].bitcast(F32),
                                  ALU.subtract).then_inc(m_lo_done, 1)

            turned = tr_ps[:, :].rearrange("p (j i w) -> p j i w", j=UG * ST, i=PAIRS)

            def invert(u):
                dve.wait_ge(o_turned, u + 1)
                dve.reciprocal(rden[:, :, :], turned[:, :, :, D]).then_inc(rden_done, 1)

            def divide(u, k, g):
                dve.wait_ge(rden_done, u + 1)
                mul = dve.tensor_tensor(attn_units[:, k, g], turned[:, ST * g:ST * g + ST, :, 0:D],
                                        rden[:, ST * g:ST * g + ST, :].unsqueeze(3).broadcast_to([P, ST, PAIRS, D]),
                                        ALU.mult)
                if g == UG - 1:
                    mul.then_inc(o_normed, 1)

            def fill_zero_row(k):
                dve.memset(q_st[k][ZROW:SROWS, :, :].bitcast(F32), 0.0).then_inc(padded, 1)

            fill_zero_row(0)
            for t in range(ST):
                batch_moments(0, t, False)
            fill_zero_row(1)
            for h in range(2):
                dve.memset(v_aug[h][:, :, :, D + 1:VW], 0.0).then_inc(padded, 1)
                dve.memset(v_aug[h][:, :, :, D:D + 1], 1.0).then_inc(padded, 1)
            fill_zero_row(2)
            for t in range(ST):
                batch_moments(1, t, t == 0)
            fill_zero_row(3)
            dve.memset(bits[:, :], 0).then_inc(padded, 1)
            dve.wait_ge(padded, UNITS + 5)
            for k in range(2):
                for t in range(4):
                    maxima(0, k, t, False)
                round_maxima(k, k, False)
                maxima_low(k, k)

            def step(b, k, first, last):
                u = UNITS * b + k
                norming = not last and b is not NORMS
                ahead = (b, k + 2) if k < 2 else (b + 1, k - 2)
                started, maxed = not (first and k == 0), not (last and k >= 2)
                if maxed:
                    maxima(*ahead, 0, True)
                if maxed:
                    maxima(*ahead, 1, True)
                if norming and k == 0:
                    batch_moments(b + 2, 0, True)
                if norming and k == 0:
                    batch_moments(b + 2, 1, False)
                if maxed:
                    maxima(*ahead, 2, True)
                if b is NORMS and k == 2:
                    dve.wait_ge(flag_turned, 1)
                    dve.tensor_reduce(low_flag[:, :], tr_ps[0:1, 0:P], AX.X, ALU.max).then_inc(flag_done, 1)
                if maxed:
                    maxima(*ahead, 3, True)
                if started:
                    invert(u - 1)
                if maxed:
                    round_maxima(u + 2, k, True)
                if started:
                    if k == 1 and not first:
                        dve.wait_ge(x1_done, b)
                    divide(u - 1, (k - 1) % UNITS, 0)
                if maxed:
                    maxima_low(u + 2, k)
                if started:
                    divide(u - 1, (k - 1) % UNITS, 1)
                if norming and k:
                    n = WCUT[k] - WCUT[k - 1]
                    dve.wait_ge(w_in, 16 * (3 * b + k))
                    if not (first and k == 1):
                        dve.wait_ge(w_seen, 3 * b + k - 1)
                    dve.tensor_tensor(bits[:, 0:n], bits[:, 0:n], w_stage[:, WCUT[k - 1]:WCUT[k]].bitcast(I32),
                                      ALU.bitwise_or).then_inc(w_seen, 1)
                if b is NORMS and k == 0:
                    dve.wait_ge(w_seen, 3 * WPIECES)
                    dve.tensor_scalar(low_bits[:, :], bits[:, :], LOW_BITS, None, ALU.bitwise_and).then_inc(flag_step, 1)
                    dve.wait_ge(flag_step, 1)
                    dve.tensor_reduce(low_col[:, :], low_bits[:, :], AX.X, ALU.max).then_inc(flag_step, 1)

            for k in range(UNITS):
                step(0, k, True, False)
            dve.wait_ge(scales_in, 48)
            dve.tensor_scalar(half_gs[:, :], gs_col[:, :], 0.5, None, ALU.mult).then_inc(scales_done, 1)
            dve.wait_ge(scales_done, 1)
            dve.tensor_tensor(hid_scale[:, :], half_gs[:, :], us_col[:, :], ALU.mult).then_inc(scales_done, 1)
            dve.wait_ge(tanh_done, 1)
            dve.tensor_scalar(down_gate[:, :], down_row[:, :], tgates[:, 1:2], None, ALU.mult).then_inc(scales_done, 1)
            with dve.Fori(1, NORMS) as b:
                for k in range(UNITS):
                    step(b, k, False, False)

            def chunk_moments(c, t):
                dve.wait_ge(c_in, 16 * (c + 1))
                if t == 0:
                    dve.wait_ge(x_normed, ST * B)
                tile_moments(c_ln, t, ST * B + CT * c + t, t)

            def rows_low(c, m, slot):
                dve.wait_ge(c_hi_done, 2 * c + m + 1)
                dve.tensor_tensor(xt_lo[:, 2 * m:2 * m + 2, :], gu_ps[slot][:, :, :],
                                  xt_hi[:, 2 * m:2 * m + 2, :].bitcast(F32), ALU.subtract).then_inc(c_lo_done, 1)

            def hidden(c, i):
                n = IT * c + i
                slot = i % 2
                hs = i % HS
                dve.wait_ge(th_done, n + 1)
                dve.scalar_tensor_tensor(silu2[slot][:, :], th[slot][:, :], 1.0, gu_ps[slot][:, 0, :],
                                         ALU.add, ALU.mult).then_inc(silu_done, 1)
                dve.wait_ge(silu_done, n + 1)
                if i >= HS:
                    dve.wait_ge(hid_lo_done, n - HS + 1)
                dve.scalar_tensor_tensor(hid[hs][:, :], silu2[slot][:, :], hid_scale[:, i:i + 1], gu_ps[slot][:, 1, :],
                                         ALU.mult, ALU.mult).then_inc(hid_done, 1)

            def output(c):
                dve.wait_ge(cr_in, 16 * (c + 1))
                for t in range(CT):
                    dve.wait_ge(acc_done, CT * c + t + 1)
                    dve.tensor_tensor(y_sb[:, t, :], acc_ps[t][:, :], down_gate[:, :], ALU.mult).then_inc(y_done, 1)

            def add_residual(c, t):
                dve.wait_ge(y_done, CT * c + t + 1)
                dve.tensor_tensor(y_sb[:, t, :], y_sb[:, t, :], c_res[:, t, :], ALU.add).then_inc(last_ready, 1)

            def chunk(c, last):
                for i in range(IT):
                    hidden(c, i)
                    if not last and 3 <= i < 3 + CT:
                        chunk_moments(c + 1, i - 3)
                if not last:
                    rows_low(c + 1, 0, 1)
                    rows_low(c + 1, 1, 0)
                output(c)
                if last:
                    for t in range(CT // 2, CT):
                        add_residual(c, t)

            for b in (NORMS, LAST):
                for k in range(UNITS):
                    step(b, k, False, b == LAST)
                    if b is NORMS and k >= 2:
                        for t in range(2 * k - 4, 2 * k - 2):
                            chunk_moments(0, t)
                    if b == LAST and k == 2:
                        rows_low(0, 0, 1)
                        rows_low(0, 1, 0)
            invert(UNITS * B - 1)
            for g in range(UG):
                divide(UNITS * B - 1, UNITS - 1, g)

            with dve.Fori(0, NCH - 1) as c:
                chunk(c, False)
            chunk(NCH - 1, True)

        @block.scalar
        def _(act):
            def queries_high(b, c, reused):
                act.wait_ge(qt_copied, 2 * b + c + 1)
                if reused:
                    act.wait_ge(qt_stored[c], 16 * b)
                act.activation(qt_parts[c][:, 0, :, :], qt[:, :, :], ACT.Copy).then_inc(qt_hi_done, 1)

            def copy_queries(b, c):
                act.wait_ge(qt_turned, 2 * b + c + 1)
                if not (isinstance(b, int) and b == 0 and c == 0):
                    act.wait_ge(qt_lo_done, 2 * b + c)
                act.activation(qt[:, :, :], tr_ps[:, :].rearrange("p (j s) -> p j s", j=2), ACT.Copy).then_inc(qt_copied, 1)

            def copy_maxima(u, k, reused):
                act.wait_ge(m_turned, u + 1)
                if reused:
                    act.wait_ge(m_in, 16 * (u - 1))
                act.activation(m_rows[k % 2][:, :], tr_ps[0:2 * UH * ST, 0:P], ACT.Copy).then_inc(m_copied, 1)

            def exponents(u, j, reused):
                tt, i = divmod(j, PAIRS)
                act.wait_ge(t_done, 2 * PAIRS * u + j + 1)
                if i == 0 and reused:
                    act.wait_ge(pv_done, TT * (u - 1) + tt + 1)
                act.activation(probs[:, tt, i, :], t_ps[j % 2][:, :], ACT.Exp, scale=RSCALE).then_inc(exp_done, 1)

            def copy_output(u):
                act.wait_ge(pv_done, TT * (u + 1))
                act.activation(o_sb[:, :], o_ps[:, :], ACT.Copy).then_inc(o_copied, 1)

            for b in range(2):
                for c in range(2):
                    copy_queries(b, c)
                    queries_high(b, c, b == 1)
                    if b and c == 0:
                        copy_maxima(0, 0, False)
            act.wait_ge(gates_in, 32)
            act.activation(tgates[:, :], gates[:, :], ACT.Tanh).then_inc(tanh_done, 1)

            def rows_high(c, m, slot):
                act.wait_ge(c_turned, 2 * c + m + 1)
                act.activation(xt_hi[:, 2 * m:2 * m + 2, :], gu_ps[slot][:, :, :], ACT.Copy).then_inc(c_hi_done, 1)

            def step(b, k, first, last):
                u = UNITS * b + k
                started = not (first and k == 0)
                norming = not last and b is not NORMS
                exponents(u, 0, started)
                exponents(u, 1, started)
                if started:
                    copy_output(u - 1)
                exponents(u, 2, started)
                exponents(u, 3, started)
                if last and k == 2:
                    for h in range(2):
                        act.wait_ge(qt_stored[h], 16 * B)
                    rows_high(0, 0, 1)
                if not (last and k == 3):
                    copy_maxima(u + 1, k + 1, started)
                exponents(u, 4, started)
                exponents(u, 5, started)
                if norming and k >= 2:
                    copy_queries(b + 2, k - 2)
                exponents(u, 6, started)
                exponents(u, 7, started)
                if last and k == 2:
                    rows_high(0, 1, 0)
                if norming and k >= 2:
                    queries_high(b + 2, k - 2, True)

            for k in range(UNITS):
                step(0, k, True, False)
            with act.Fori(1, NORMS) as b:
                for k in range(UNITS):
                    step(b, k, False, False)

            def half_tanh(c, i):
                act.wait_ge(gu_done, IT * c + i + 1)
                act.activation(th[i % 2][:, :], gu_ps[i % 2][:, 0, :], ACT.Tanh,
                               scale=half_gs[:, i:i + 1]).then_inc(th_done, 1)

            def hidden_high(c, i):
                n = IT * c + i
                act.wait_ge(hid_done, n + 1)
                if i >= HS:
                    act.wait_ge(down_done, (IT - 1) * c + i - HS + 1)
                act.activation(hid_hi[i % HS][:, :], hid[i % HS][:, :], ACT.Copy).then_inc(hid_hi_done, 1)

            def chunk(c, last):
                for i in range(IT):
                    if i:
                        hidden_high(c, i - 1)
                    half_tanh(c, i)
                hidden_high(c, IT - 1)
                if not last:
                    rows_high(c + 1, 0, 1)
                    rows_high(c + 1, 1, 0)

            for b in (NORMS, LAST):
                for k in range(UNITS):
                    step(b, k, False, b == LAST)
            copy_output(UNITS * B - 1)

            with act.Fori(0, NCH - 1) as c:
                chunk(c, False)
            chunk(NCH - 1, True)

        @block.tensor
        def _(pe):
            def turn_queries(b, c):
                pe.wait_ge(x_normed, ST * (b + 1))
                for j in range(2):
                    for st in range(ST):
                        at = j * S + st * P
                        mm = pe.transpose(tr_ps[:, at:at + P], x_norm[:, st, (2 * c + j) * P:(2 * c + j + 1) * P], ident[:, :])
                mm.then_inc(qt_turned, 1)

            def scores(b, k, t, reused):
                u = UNITS * b + k
                h = k // 2
                if t == 0:
                    pe.wait_ge(q_in[k], 32 * (b + 1))
                    pe.wait_ge(k_max_done, 2 * b + h + 1)
                if reused:
                    pe.wait_ge(max_done, PAIRS * u + t - 1)
                for g in range(UG):
                    for st in range(ST):
                        mm = pe.matmul(s_ps[t % 2][:, ST * g + st, :], q_st[k][0:SROWS, UG * t + g, st * P:(st + 1) * P],
                                       k_max[h][0:SROWS, kv_of(k, t), :], start=True, stop=True)
                mm.then_inc(s_done, 1)

            def turn_maxima(u, k):
                pe.wait_ge(m_lo_done, u + 1)
                pe.transpose(tr_ps[0:2 * UH * ST, 0:P], m_parts[k % 2][:, :, :].rearrange("p a n -> p (a n)").bitcast(F32),
                             ident[:, :]).then_inc(m_turned, 1)

            def shifted(b, k, j, reused):
                u = UNITS * b + k
                h = k // 2
                tt, i = divmod(j, PAIRS)
                if j == 0:
                    pe.wait_ge(m_in, 16 * (u + 1))
                    pe.wait_ge(k_exp_done, 2 * b + h + 1)
                if reused:
                    pe.wait_ge(exp_done, 2 * PAIRS * u + j - 1)
                pe.matmul(t_ps[j % 2][:, :], k_exp[h][0:DROWS, kv_of(k, i), tt * P:(tt + 1) * P],
                          q_st[k][0:DROWS, UG * i:UG * i + UG, :].rearrange("p g s -> p (g s)"),
                          start=True, stop=True).then_inc(t_done, 1)

            def weigh(b, k, tt, reused):
                u = UNITS * b + k
                h = k // 2
                pe.wait_ge(exp_done, 2 * PAIRS * u + PAIRS * (tt + 1))
                if tt == 0:
                    pe.wait_ge(v_done, TT * (2 * b + h + 1))
                    if reused:
                        pe.wait_ge(o_copied, u)
                for i in range(PAIRS):
                    mm = pe.matmul(o_ps[i * VW:(i + 1) * VW, :], v_aug[h][:, tt, kv_of(k, i), :], probs[:, tt, i, :],
                                   start=(tt == 0), stop=(tt == TT - 1))
                mm.then_inc(pv_done, 1)

            def turn_output(u):
                pe.wait_ge(o_copied, u + 1)
                for j in range(UG * ST):
                    mm = pe.transpose(tr_ps[:, j * P:(j + 1) * P], o_sb[:, j * P:(j + 1) * P], ident[:, :])
                mm.then_inc(o_turned, 1)

            def turn_rows(c, m, slot):
                pe.wait_ge(c_normed, CT * (c + 1))
                for kk in range(2):
                    for t in range(CT):
                        k = 2 * m + kk
                        mm = pe.transpose(gu_ps[slot][:, kk, t * P:(t + 1) * P], c_norm[:, t, k * P:(k + 1) * P],
                                          ident[:, :])
                mm.then_inc(c_turned, 1)

            pe.wait_ge(ident_done, 1)
            turn_queries(0, 0)
            pe.wait_ge(qt_copied, 1)
            turn_queries(0, 1)

            def keep_busy(n):
                for _ in range(n):
                    pe.matmul(t_ps[0][:, 0:P], ident[:, :], ident[:, :], start=True, stop=True)

            keep_busy(WARMUP)
            pe.wait_ge(filled, 6)
            pe.wait_ge(padded, UNITS + 5)
            for t in range(PAIRS):
                scores(0, 0, t, t >= 2)
                keep_busy(BUSY)
                if t == 0:
                    pe.wait_ge(qt_copied, 2)
                    turn_queries(1, 0)
            pe.wait_ge(qt_copied, 3)
            for t in range(PAIRS):
                scores(0, 1, t, True)
                keep_busy(BUSY)
                if t == 0:
                    turn_maxima(0, 0)
            pe.wait_ge(m_copied, 1)
            turn_queries(1, 1)

            def step(b, k, first, last, between=None):
                u = UNITS * b + k
                norming = not last and b is not NORMS
                ahead = (b, k + 2) if k < 2 else (b + 1, k - 2)
                started = not (first and k == 0)
                scored = not (last and k >= 2)
                before = (b, k - 1) if k else (b - 1, UNITS - 1)
                shifted(b, k, 0, started)
                shifted(b, k, 1, started)
                if started:
                    weigh(*before, 1, True)
                shifted(b, k, 2, True)
                if scored:
                    scores(*ahead, 0, True)
                shifted(b, k, 3, True)
                if last and k == 2:
                    pe.wait_ge(max_done, PAIRS * UNITS * B)
                    turn_rows(0, 0, 1)
                if scored:
                    scores(*ahead, 1, True)
                shifted(b, k, 4, True)
                if not (last and k == 3):
                    if first and k == 0:
                        pe.wait_ge(qt_copied, 4)
                    elif first and k == 1:
                        pe.wait_ge(m_copied, 2)
                    else:
                        pe.wait_ge(o_normed, u - 1)
                    turn_maxima(u + 1, k + 1)
                shifted(b, k, 5, True)
                weigh(b, k, 0, started)
                if between:
                    between(0)
                if norming and k >= 2:
                    pe.wait_ge(m_copied, u + 2)
                    turn_queries(b + 2, k - 2)
                if b is NORMS and k == 2:
                    pe.wait_ge(m_copied, u + 2)
                    pe.wait_ge(flag_step, 2)
                    pe.transpose(tr_ps[0:1, 0:P], low_col[:, :], ident[:, :]).then_inc(flag_turned, 1)
                shifted(b, k, 6, True)
                if between:
                    between(1)
                if scored:
                    scores(*ahead, 2, True)
                shifted(b, k, 7, True)
                if last and k == 2:
                    turn_rows(0, 1, 0)
                if between:
                    between(2)
                if scored:
                    scores(*ahead, 3, True)
                if started:
                    if norming and k >= 2:
                        pe.wait_ge(qt_copied, 2 * (b + 2) + k - 1)
                    elif b is NORMS and k == 2:
                        pe.wait_ge(flag_done, 1)
                    elif last and k == 3:
                        pe.wait_ge(o_normed, u - 1)
                    else:
                        pe.wait_ge(m_copied, u + 2)
                    turn_output(u - 1)
                if between:
                    between(3)

            for k in range(UNITS):
                step(0, k, True, False)
            with pe.Fori(1, NORMS) as b:
                for k in range(UNITS):
                    step(b, k, False, False)
            for b in (NORMS, LAST):
                for k in range(UNITS - (b == LAST)):
                    step(b, k, False, b == LAST)

            def free_slots(c, used):
                if used <= 2:
                    pe.wait_ge(c_lo_done, 2 * c + used)
                else:
                    pe.wait_ge(hid_done, IT * c + used - 2)

            def feed_forward(kind):
                def as_kind(ap):
                    return ap if kind == F32R else ap.bitcast(kind)

                def gate_up(c, i, quarters=range(4)):
                    slot = i % 2
                    if 0 in quarters:
                        free_slots(c, 2 if i == 0 else i + 1)
                    for q in quarters:
                        half, w = ((0, gate_w), (1, up_w))[q // 2]
                        for k in range(2 * (q % 2), 2 * (q % 2) + 2):
                            for part in (xt_hi, xt_lo):
                                mm = pe.matmul(gu_ps[slot][:, half, :], as_kind(w[:, k, i * P:(i + 1) * P]),
                                               as_kind(part[:, k, :]), start=(k == 0 and part is xt_hi),
                                               stop=(k == KT - 1 and part is xt_lo))
                    if 3 in quarters:
                        mm.then_inc(gu_done, 1)

                def down(c, i):
                    for part, done in ((hid_hi, hid_hi_done), (hid_lo, hid_lo_done)):
                        pe.wait_ge(done, IT * c + i + 1)
                        for t in range(CT):
                            mm = pe.matmul(acc_ps[t][:, :], as_kind(part[i % HS][:, t * P:(t + 1) * P]),
                                           as_kind(down_w[:, i, :]), start=(i == 0 and part is hid_hi),
                                           stop=(i == IT - 1 and part is hid_lo))
                            if i == IT - 1 and part is hid_lo:
                                mm.then_inc(acc_done, 1)
                    if i < IT - 1:
                        mm.then_inc(down_done, 1)

                def chunk(c, last):
                    for i in range(LAG, IT):
                        gate_up(c, i)
                        down(c, i - LAG)
                    if not last:
                        free_slots(c, IT + 1)
                        turn_rows(c + 1, 0, 1)
                        free_slots(c, IT + 2)
                        turn_rows(c + 1, 1, 0)
                    down(c, IT - 2)
                    down(c, IT - 1)
                    if not last:
                        for i in range(LAG):
                            gate_up(c + 1, i)

                step(LAST, UNITS - 1, False, True, lambda q: gate_up(0, 0, (q,)))
                weigh(LAST, UNITS - 1, 1, True)
                gate_up(0, 1, (0, 1))
                pe.wait_ge(o_normed, UNITS * B - 1)
                turn_output(UNITS * B - 1)
                gate_up(0, 1, (2, 3))
                with pe.Fori(0, NCH - 1) as c:
                    chunk(c, False)
                chunk(NCH - 1, True)

            pe.wait_ge(w_set, 16 * 3 * WPIECES)
            pe.wait_ge(flag_done, 1)
            inexact = pe.value_load(low_flag[0:1, 0:1])
            with pe.If(inexact == 0):
                feed_forward(F32R)
            with pe.Else():
                feed_forward(F32)


_INS = ["x", "ctx_n", "ctx_t", "g_xattn", "g_ffn", "weights", "gate_s", "up_s", "down_s"]


def kernel(x, ctx_512, g_xattn, g_ffn, L0_ffn_gate_w, L0_ffn_up_w, L0_ffn_down_w, L0_ffn_gate_s, L0_ffn_up_s,
           L0_ffn_down_s):
    import concourse.bacc as bacc
    from concourse.bass_utils import run_bass_kernel_spmd

    def rows_on_partitions(w):
        n = w.shape[0] // P
        return w.reshape(n, P, w.shape[1]).transpose(1, 0, 2).reshape(P, -1)

    ctx = np.asarray(ctx_512)
    arrays = {
        "x": np.asarray(x), "ctx_n": ctx, "ctx_t": ctx.reshape(B * T, KV * D).T,
        "g_xattn": np.asarray(g_xattn), "g_ffn": np.asarray(g_ffn),
        "weights": np.concatenate([rows_on_partitions(np.asarray(w).T)
                                   for w in (L0_ffn_gate_w, L0_ffn_up_w, L0_ffn_down_w)], axis=1),
        "gate_s": np.asarray(L0_ffn_gate_s).reshape(IT, P).T, "up_s": np.asarray(L0_ffn_up_s).reshape(IT, P).T,
        "down_s": np.asarray(L0_ffn_down_s),
    }
    nc = bacc.Bacc("TRN2", target_bir_lowering=False, num_devices=1)
    args = []
    for name in _INS:
        arrays[name] = np.ascontiguousarray(arrays[name])
        args.append(nc.dram_tensor(name, arrays[name].shape, F32, kind="ExternalInput").ap())
    out = nc.dram_tensor("out", [B, S, E], F32, kind="ExternalOutput").ap()
    build(nc, *args, out)
    r = run_bass_kernel_spmd(nc, [arrays], core_ids=[0])
    return r.results[0]["out"]
```
